# Optimizing a Trainium2 kernel written in Bass

```python
import numpy as np
import jax
import jax.numpy as jnp

def _softmax(x, axis=-1):
    return jax.nn.softmax(x, axis=axis)

def _gelu(x):
    return jax.nn.gelu(x, approximate=True)

def _silu(x):
    return jax.nn.silu(x)

def _sigmoid(x):
    return jax.nn.sigmoid(x)

def _layernorm(x, axis=-1, eps=1e-05):
    m = jnp.mean(x, axis=axis, keepdims=True)
    v = jnp.var(x, axis=axis, keepdims=True)
    return (x - m) / jnp.sqrt(v + eps)

def _scatter_add(tgt, idx, src, axis=0):
    return tgt.at[idx].add(src)

def _segment_sum(src, seg, n):
    return jax.ops.segment_sum(src, seg, n)
kernel_name = 'mk_adaln_d2_jaxref_r8_c28d15'

def setup_inputs(seed: int=0):
    np.random.seed(seed)
    _w = jnp.asarray

    def _L0_attn_setup():
        import jax, jax.numpy as jnp
        import numpy as np
        B, L, D = (8, 512, 128)
        key = jax.random.key(seed)
        k1, k2, k3, k4, k5 = jax.random.split(key, 5)
        s = 1.0 / np.sqrt(D)
        return {'x': jax.random.normal(k1, (B, L, D), dtype=jnp.float32), 'Wg': jax.random.uniform(k2, (1, D), dtype=jnp.float32, minval=-s, maxval=s), 'bg': jax.random.uniform(k3, (1,), dtype=jnp.float32, minval=-s, maxval=s), 'Wout': jax.random.uniform(k4, (D, D), dtype=jnp.float32, minval=-s, maxval=s), 'bout': jax.random.uniform(k5, (D,), dtype=jnp.float32, minval=-s, maxval=s)}
    _L0_attn_in = _L0_attn_setup()

    def _L0_ffn_setup():
        import jax, jax.numpy as jnp
        import numpy as np
        D_MODEL, D_FF, D2, DL = (128, 512, 64, 64)
        D1 = D_FF // D2
        BATCH, SEQ = (2, 128)
        KERNEL_SCALE = D2 ** 0.5
        key = jax.random.key(seed)
        ks = jax.random.split(key, 7)
        xav = lambda k, shape, fan: jax.random.normal(k, shape, jnp.float32) * (2.0 / sum(fan)) ** 0.5
        x = jax.random.normal(ks[0], (BATCH, SEQ, D_MODEL), jnp.float32)
        m1 = xav(ks[1], (D_MODEL, DL), (D_MODEL, DL))
        m2 = xav(ks[2], (DL, D1, D2), (DL, D_FF))
        mb = jax.random.normal(ks[3], (D1, D2), jnp.float32)
        w1 = xav(ks[4], (D_MODEL, D1, D2), (D_MODEL, D_FF))
        w2 = xav(ks[5], (D2, D1, D_MODEL), (D_FF, D_MODEL)) * KERNEL_SCALE
        b2 = jax.random.normal(ks[6], (D_MODEL,), jnp.float32)
        return {'x': x, 'm1': m1, 'm2': m2, 'mb': mb, 'w1': w1, 'w2': w2, 'b2': b2}
    _L0_ffn_in = _L0_ffn_setup()
    _L0_c = _w((lambda *s: np.random.randn(*s).astype(np.float32) * 0.05)(16, 128))
    _L0_wmod = _w((lambda *s: np.random.randn(*s).astype(np.float32) * 0.05)(128, 6 * 128) * 128 ** (-0.5))

    def _L1_attn_setup():
        import jax, jax.numpy as jnp
        import numpy as np
        B, T, D = (4, 256, 128)
        NUM_HEADS, HEAD_DIM = (16, 64)
        ROPE_THETA = 10000.0

        def precompute_freqs_cis(dim, max_seq_len, theta=10000.0):
            inv_freq = 1.0 / theta ** (jnp.arange(0, dim, 2, dtype=jnp.float32) / dim)
            freqs = jnp.outer(jnp.arange(max_seq_len, dtype=jnp.float32), inv_freq)
            return (jnp.cos(freqs), jnp.sin(freqs))

        def apply_rotary_emb(x, cos, sin):
            c = cos[None, None, :, :]
            s = sin[None, None, :, :]
            x1, x2 = jnp.split(x.astype(jnp.float32), 2, axis=-1)
            return jnp.concatenate([x1 * c - x2 * s, x1 * s + x2 * c], axis=-1).astype(x.dtype)
        key = jax.random.key(seed)
        ks = jax.random.split(key, 5)
        scale = 1.0 / np.sqrt(D)
        return {'x': jax.random.normal(ks[0], (B, T, D), dtype=jnp.float32), 'wq': jax.random.normal(ks[1], (NUM_HEADS * HEAD_DIM, D), dtype=jnp.float32) * scale, 'wk': jax.random.normal(ks[2], (NUM_HEADS * HEAD_DIM, D), dtype=jnp.float32) * scale, 'wv': jax.random.normal(ks[3], (NUM_HEADS * HEAD_DIM, D), dtype=jnp.float32) * scale, 'wo': jax.random.normal(ks[4], (D, NUM_HEADS * HEAD_DIM), dtype=jnp.float32) * scale}
    _L1_attn_in = _L1_attn_setup()

    def _L1_ffn_setup():
        import jax, jax.numpy as jnp
        import numpy as np
        D_MODEL, D_FF, RANK = (128, 512, 32)
        B, S = (4, 512)
        key = jax.random.key(seed)
        ks = jax.random.split(key, 7)
        return {'x': jax.random.normal(ks[0], (B, S, D_MODEL), dtype=jnp.float32), 'U1': jax.random.normal(ks[1], (D_MODEL, RANK), dtype=jnp.float32) * 0.02, 'V1': jax.random.normal(ks[2], (RANK, D_FF), dtype=jnp.float32) * 0.02, 'b1': jnp.zeros((D_FF,), dtype=jnp.float32), 'U2': jax.random.normal(ks[3], (D_FF, RANK), dtype=jnp.float32) * 0.02, 'V2': jax.random.normal(ks[4], (RANK, D_MODEL), dtype=jnp.float32) * 0.02, 'b2': jnp.zeros((D_MODEL,), dtype=jnp.float32)}
    _L1_ffn_in = _L1_ffn_setup()
    _L1_c = _w((lambda *s: np.random.randn(*s).astype(np.float32) * 0.05)(16, 128))
    _L1_wmod = _w((lambda *s: np.random.randn(*s).astype(np.float32) * 0.05)(128, 6 * 128) * 128 ** (-0.5))
    _d = {'L0_attn_x': _L0_attn_in['x'], 'L0_attn_Wg': _L0_attn_in['Wg'], 'L0_attn_bg': _L0_attn_in['bg'], 'L0_attn_Wout': _L0_attn_in['Wout'], 'L0_attn_bout': _L0_attn_in['bout'], 'L0_ffn_m1': _L0_ffn_in['m1'], 'L0_ffn_m2': _L0_ffn_in['m2'], 'L0_ffn_mb': _L0_ffn_in['mb'], 'L0_ffn_w1': _L0_ffn_in['w1'], 'L0_ffn_w2': _L0_ffn_in['w2'], 'L0_ffn_b2': _L0_ffn_in['b2'], 'L0_c': _L0_c, 'L0_wmod': _L0_wmod, 'L1_attn_wq': _L1_attn_in['wq'], 'L1_attn_wk': _L1_attn_in['wk'], 'L1_attn_wv': _L1_attn_in['wv'], 'L1_attn_wo': _L1_attn_in['wo'], 'L1_ffn_U1': _L1_ffn_in['U1'], 'L1_ffn_V1': _L1_ffn_in['V1'], 'L1_ffn_b1': _L1_ffn_in['b1'], 'L1_ffn_U2': _L1_ffn_in['U2'], 'L1_ffn_V2': _L1_ffn_in['V2'], 'L1_ffn_b2': _L1_ffn_in['b2'], 'L1_c': _L1_c, 'L1_wmod': _L1_wmod}
    _x0 = _d['L0_attn_x']
    _d['L0_attn_x'] = jax.random.normal(jax.random.fold_in(jax.random.key(seed), 1), (16, 256, 128), dtype=_x0.dtype)
    del _x0
    return _d

def reference(L0_attn_x, L0_attn_Wg, L0_attn_bg, L0_attn_Wout, L0_attn_bout, L0_ffn_m1, L0_ffn_m2, L0_ffn_mb, L0_ffn_w1, L0_ffn_w2, L0_ffn_b2, L0_c, L0_wmod, L1_attn_wq, L1_attn_wk, L1_attn_wv, L1_attn_wo, L1_ffn_U1, L1_ffn_V1, L1_ffn_b1, L1_ffn_U2, L1_ffn_V2, L1_ffn_b2, L1_c, L1_wmod):

    def _L0_attn_ref(x, Wg, bg, Wout, bout):
        import jax, jax.numpy as jnp
        import numpy as np
        B, L, D = (8, 512, 128)
        g = jax.nn.sigmoid(jnp.einsum('bld,d->bl', x, Wg[0]) + bg[0])
        g_t = jnp.transpose(g)[:, :, None]
        x_t = jnp.transpose(x, (1, 0, 2))
        h0 = jnp.zeros((x.shape[0], x.shape[2]), dtype=x.dtype)

        def step(h, inp):
            gt, xt = inp
            h = (1.0 - gt) * h + gt * xt
            return (h, h)
        _, hs = jax.lax.scan(step, h0, (g_t, x_t))
        H = jnp.transpose(hs, (1, 0, 2))
        out = jnp.einsum('bld,ed->ble', H, Wout) + bout
        return out

    def _L0_ffn_ref(x, m1, m2, mb, w1, w2, b2):
        import jax, jax.numpy as jnp
        import numpy as np
        D_MODEL, D_FF, D2, DL = (128, 512, 64, 64)
        D1 = D_FF // D2
        BATCH, SEQ = (2, 128)
        KERNEL_SCALE = D2 ** 0.5
        x_shape = x.shape
        xf = x.reshape(-1, x_shape[-1])
        d1 = w1.shape[1]
        lr = xf @ m1
        mask_logits = jnp.einsum('bl,lxy->bxy', lr, m2) + mb
        quant_mask = jnp.argmax(mask_logits, axis=-1)
        w1p = jnp.transpose(w1, (1, 2, 0))
        w2p = jnp.transpose(w2, (1, 0, 2))
        j = jnp.arange(d1)[None, :]
        w = w1p[j, quant_mask]
        mid = jnp.einsum('ai,aji->aj', xf, w)
        relu = jax.nn.relu(mid)
        v = w2p[j, quant_mask]
        res = jnp.einsum('ai,aij->aj', relu, v) + b2
        return res.reshape(x_shape)

    def _L1_attn_ref(x, wq, wk, wv, wo):
        import jax, jax.numpy as jnp
        import numpy as np
        B, T, D = (4, 256, 128)
        NUM_HEADS, HEAD_DIM = (16, 64)
        ROPE_THETA = 10000.0

        def precompute_freqs_cis(dim, max_seq_len, theta=10000.0):
            inv_freq = 1.0 / theta ** (jnp.arange(0, dim, 2, dtype=jnp.float32) / dim)
            freqs = jnp.outer(jnp.arange(max_seq_len, dtype=jnp.float32), inv_freq)
            return (jnp.cos(freqs), jnp.sin(freqs))

        def apply_rotary_emb(x, cos, sin):
            c = cos[None, None, :, :]
            s = sin[None, None, :, :]
            x1, x2 = jnp.split(x.astype(jnp.float32), 2, axis=-1)
            return jnp.concatenate([x1 * c - x2 * s, x1 * s + x2 * c], axis=-1).astype(x.dtype)
        batch, seq_len, _ = x.shape
        q = jnp.einsum('btd,od->bto', x, wq, preferred_element_type=jnp.float32)
        k = jnp.einsum('btd,od->bto', x, wk, preferred_element_type=jnp.float32)
        v = jnp.einsum('btd,od->bto', x, wv, preferred_element_type=jnp.float32)
        q = q.reshape(batch, seq_len, NUM_HEADS, HEAD_DIM).transpose(0, 2, 1, 3)
        k = k.reshape(batch, seq_len, NUM_HEADS, HEAD_DIM).transpose(0, 2, 1, 3)
        v = v.reshape(batch, seq_len, NUM_HEADS, HEAD_DIM).transpose(0, 2, 1, 3)
        cos, sin = precompute_freqs_cis(HEAD_DIM, seq_len, ROPE_THETA)
        q = apply_rotary_emb(q, cos, sin)
        k = apply_rotary_emb(k, cos, sin)
        scale = jnp.asarray(HEAD_DIM ** (-0.5), dtype=jnp.float32)
        scores = jnp.einsum('bhid,bhjd->bhij', q, k, preferred_element_type=jnp.float32) * scale
        causal = jnp.tril(jnp.ones((seq_len, seq_len), dtype=bool))
        scores = jnp.where(causal, scores, -jnp.inf)
        probs = jax.nn.softmax(scores, axis=-1).astype(x.dtype)
        out = jnp.einsum('bhij,bhjd->bhid', probs, v, preferred_element_type=jnp.float32).astype(x.dtype)
        out = out.transpose(0, 2, 1, 3).reshape(batch, seq_len, NUM_HEADS * HEAD_DIM)
        out = jnp.einsum('btd,od->bto', out, wo, preferred_element_type=jnp.float32)
        return out

    def _L1_ffn_ref(x, U1, V1, b1, U2, V2, b2):
        import jax, jax.numpy as jnp
        import numpy as np
        D_MODEL, D_FF, RANK = (128, 512, 32)
        B, S = (4, 512)
        P = jnp.einsum('bsd,dr->bsr', x, U1)
        H = jax.nn.gelu(jnp.einsum('bsr,rf->bsf', P, V1) + b1)
        Q = jnp.einsum('bsf,fr->bsr', H, U2)
        return jnp.einsum('bsr,rd->bsd', Q, V2) + b2
    x = L0_attn_x
    mod = (_silu(L0_c) @ L0_wmod).reshape(L0_c.shape[0], 6, 1, -1)
    sa, ca, ga, sb, cb, gb = (mod[:, 0], mod[:, 1], mod[:, 2], mod[:, 3], mod[:, 4], mod[:, 5])
    ga = (2 * (ga >= 0) - 1) * jnp.maximum(jnp.abs(ga), 0.25)
    gb = (2 * (gb >= 0) - 1) * jnp.maximum(jnp.abs(gb), 0.25)
    h = _layernorm(x, axis=-1) * (1 + ca) + sa
    x = x + ga * _L0_attn_ref(h, L0_attn_Wg, L0_attn_bg, L0_attn_Wout, L0_attn_bout)
    h = _layernorm(x, axis=-1) * (1 + cb) + sb
    x = x + gb * _L0_ffn_ref(h, L0_ffn_m1, L0_ffn_m2, L0_ffn_mb, L0_ffn_w1, L0_ffn_w2, L0_ffn_b2)
    mod = (_silu(L1_c) @ L1_wmod).reshape(L1_c.shape[0], 6, 1, -1)
    sa, ca, ga, sb, cb, gb = (mod[:, 0], mod[:, 1], mod[:, 2], mod[:, 3], mod[:, 4], mod[:, 5])
    ga = (2 * (ga >= 0) - 1) * jnp.maximum(jnp.abs(ga), 0.25)
    gb = (2 * (gb >= 0) - 1) * jnp.maximum(jnp.abs(gb), 0.25)
    h = _layernorm(x, axis=-1) * (1 + ca) + sa
    x = x + ga * _L1_attn_ref(h, L1_attn_wq, L1_attn_wk, L1_attn_wv, L1_attn_wo)
    h = _layernorm(x, axis=-1) * (1 + cb) + sb
    x = x + gb * _L1_ffn_ref(h, L1_ffn_U1, L1_ffn_V1, L1_ffn_b1, L1_ffn_U2, L1_ffn_V2, L1_ffn_b2)
    return x

_drawn_inputs = setup_inputs


def setup_inputs(seed=0):
    import zlib

    import numpy as np

    out = dict(_drawn_inputs(seed))
    spreads = {'L1_ffn_b1': (0.0, 0.8), 'L1_ffn_b2': (0.0, 0.322)}
    factors = {'L0_attn_bout': 2.699,
     'L1_ffn_U1': 8.0,
     'L1_ffn_V1': 8.0,
     'L1_ffn_U2': 8.0,
     'L1_ffn_V2': 8.0}
    for name, (base, spread) in spreads.items():
        noise = np.random.default_rng([zlib.crc32(name.encode()), seed]).standard_normal(out[name].shape)
        drawn = base * np.exp(spread * noise) if base else spread * noise
        out[name] = jnp.asarray(drawn.astype(out[name].dtype))
    for name, factor in factors.items():
        out[name] = (out[name] * factor).astype(out[name].dtype)
    return out
```

```python
from contextlib import ExitStack

import numpy as np
import concourse.bass as bass
from concourse import mybir

ALU = mybir.AluOpType
ACT = mybir.ActivationFunctionType
AX_X = mybir.AxisListType.X
F32 = mybir.dt.float32
F32R = mybir.dt.float32r
BF16 = mybir.dt.bfloat16
F16 = mybir.dt.float16

P = 128
B, T, D = 16, 256, 128
NT = T // P
TILES = B * NT
F = 512
FC = F // P
GROUPS, PICK = 8, 64
H, DH = 16, 64
HALF = DH // 2
PAIRS = H // 2
EPS = 1e-5
ROOT_STEPS = 12
P_SCALE = 4096.0
WIDE = 4


class Signal:

    def __init__(self, ctx, nc, name, per_batch):
        self.sem = ctx.enter_context(nc.semaphore(name))
        self.per = per_batch

    def nth(self, t, n):
        return t * self.per + (self.per + n)

    def before(self, t, n):
        return t * self.per + n


def program(nc, a, out):
    ctx = ExitStack()
    with ctx:
        def sb(name, shape, dt=F32):
            return ctx.enter_context(nc.sbuf_tensor(name, shape, dt))

        def sem(name):
            return ctx.enter_context(nc.semaphore(name))

        signals = []

        def sig(name, per):
            signals.append(Signal(ctx, nc, name, per))
            return signals[-1]

        bank = [ctx.enter_context(nc.psum_tensor(f"bank{i}", [P, 512], F32)) for i in range(8)]

        x = sb("x", [P, TILES, D])
        ident = sb("ident", [P, P])
        ident_bf = sb("ident_bf", [P, P], BF16)
        causal = sb("causal", [P, P])
        causal_bf = sb("causal_bf", [P, P], BF16)
        first = sb("first", [P, P])
        first_bf = sb("first_bf", [P, P], BF16)
        rope_tab = sb("rope_tab", [P, 4, T])
        ones_row = sb("ones_row", [1, P])
        cT = sb("cT", [P, 2, B])
        silu = sb("silu", [P, 2, B])
        silu_e = sb("silu_e", [P, 2, B])
        wmod = sb("wmod", [P, 2, 6 * D])
        modT = sb("modT", [P, 2, 4, B])
        gate_row = sb("gate_row", [B, 2, 2, D])
        gate = sb("gate", [P, 2, 2, B, D])
        gates0 = gate[:, 0, :, :, :].rearrange("p k r d -> p (k r d)")
        wg = sb("wg", [P, 1])
        bg = sb("bg", [P, 1])
        nbg = sb("nbg", [P, 1])
        woutT = sb("woutT", [P, D])
        bias_rows = sb("bias_rows", [1, 3, D])
        mb_row = sb("mb_row", [1, F])
        m1T = sb("m1T", [DH, D])
        m2 = sb("m2", [DH, F])
        w_in = sb("w_in", [P, 2 * F])
        w_in_hi = sb("w_in_hi", [P, 2 * F], F32R)
        w_in_lo = sb("w_in_lo", [P, 2 * F], F32R)
        w2 = sb("w2", [P, FC, D])
        stage = sb("stage", [P, 2, H * DH])
        w_hi = sb("w_hi", [P, 5, H * DH], F32R)
        w_lo = sb("w_lo", [P, 5, H * DH], F32R)
        woT = sb("woT", [P, PAIRS, D])
        u1T = sb("u1T", [32, D])
        v1 = sb("v1", [32, F])
        u2T = sb("u2T", [32, F])
        v2 = sb("v2", [32, D])
        b1 = sb("b1", [P, FC])
        uv1 = sb("uv1", [P, F])
        uv2 = sb("uv2", [P, FC, D])

        stats = sb("stats", [P, TILES, 6])
        mean = sb("mean", [P, TILES])
        apart = sb("apart", [P, TILES])
        var = sb("var", [P, TILES])
        root = sb("root", [P, TILES])
        rstd = sb("rstd", [P, TILES])
        newton = sb("newton", [P, TILES])

        xn = sb("xn", [P, WIDE, NT, D])
        hT = sb("hT", [P, WIDE, T])
        step = sb("step", [P, WIDE, NT, D])

        h_hi = sb("h_hi", [P, T], F32R)
        h_lo = sb("h_lo", [P, T], F32R)
        top = sb("top", [P, NT, GROUPS])
        hits = sb("hits", [P, NT, F], BF16)
        hitsT = sb("hitsT", [P, FC, T], BF16)
        picked = sb("picked", [P, FC, T], BF16)
        hid = sb("hid", [P, WIDE, FC, T])
        g, keep, gh, scanned = (hid[:, :, i, :] for i in range(4))
        hid_flat = hid[:, :, :, :].rearrange("p w c t -> p (w c t)")

        val1 = sb("val1", [P, NT, H, DH + 1], BF16)
        val2 = sb("val2", [P, NT, H, DH], BF16)
        val3 = sb("val3", [P, NT, H, DH], BF16)
        val_rest = sb("val_rest", [P, NT, H * DH])
        gate_hi, gate_lo, gate_a, gate_b = (
            val_rest[0:B, i // 2, (i % 2) * 512:(i % 2 + 1) * 512].rearrange("b (l k d) -> b l k d", l=2, k=2)
            for i in range(4))
        rope_a = sb("rope_a", [P, 2, 2 * T])
        rope_b = w_in[:, :].rearrange("p (b n) -> p b n", b=2)
        nmax = sb("nmax", [P, 4, NT])
        rsum = sb("rsum", [P, 2, 4])
        qk = gates0[:, 0:2048].rearrange("p (b a t) -> p b a t", b=4, a=2)
        oT = gates0[:, 2048:4096].rearrange("p (b t) -> p b t", b=PAIRS)
        probs = hid_flat[:, 0:1536].rearrange("p (b k) -> p b k", b=4)
        probsT_hi = hid_flat[:, 1536:2304].bitcast(F16).rearrange("p (b k) -> p b k", b=4)
        probsT_lo = hid_flat[:, 2304:3072].bitcast(F16).rearrange("p (b k) -> p b k", b=4)
        o = hid_flat[:, 3072:3584].rearrange("p (b j h d) -> p b j h d", b=2, j=NT, h=2)

        s_x = sem("x_loaded")
        s_const = sem("constants_loaded")
        s_w = [sem(f"attention_weights_loaded_{i}") for i in range(2)]
        s_out = sem("output_stored")
        pre_v = sem("prologue_vector")
        pre_s = sem("prologue_scalar")
        pre_t = sem("prologue_tensor")
        w_split = sem("attention_weight_split")
        st_v = sem("rstd_vector_step")
        st_s = sem("rstd_root")

        def phase(tag, **counts):
            return {k: sig(f"{tag}_{k}", v) for k, v in counts.items()}

        L1 = phase("scan", xn=WIDE, xT=WIDE, h=WIDE, z=WIDE, g=WIDE, keep=WIDE, gh=WIDE, scanned=WIDE,
                   y=WIDE, gated=WIDE, x=WIDE, stats=WIDE)
        L2 = phase("pick", xn=1, xT=1, h=1, hi=1, lo=1, logits=2, top=2, hits=2, hitsT_ps=1, hitsT=1,
                   first=1, picked=2, hidden=1, hid=2, y=1, gated=1, x=1, stats=1)
        L3 = phase("attn", xn=1, xT=1, h=1, hi=1, lo=1, v_ps=4, v1=4, rest=4, v2=4, v3=4, qk_ps=PAIRS,
                   mul=PAIRS, rope=PAIRS, s=H, nmax=H, exp=H, pT=H, pT_hi=H, pT_lo=H, pv=PAIRS,
                   rsum=PAIRS, o=PAIRS, oT_ps=PAIRS, oT=PAIRS, y=1, gated=1, x=1, stats=1)
        L4 = phase("gelu", xn=WIDE, xT=WIDE, h=WIDE, up=WIDE, act=WIDE * FC, y=WIDE, gated=WIDE, x=WIDE)

        CONSTS = [
            (ident, a["ident"]), (causal, a["causal"]), (first, a["first"]),
            (rope_tab, a["rope"]), (cT, a["cT"]), (wmod, a["wmod"]), (wg, a["wg"]), (woutT, a["woutT"]),
            (bias_rows, a["bias_rows"]), (mb_row, a["mb"]), (m1T, a["m1T"]), (m2, a["m2"]), (w2, a["w2"]),
            (woT, a["woT"]), (u1T, a["u1T"]), (v1, a["v1"]), (u2T, a["u2T"]), (v2, a["v2"]), (b1, a["b1"]),
        ]

        def full(tensor):
            return tensor[tuple(slice(None) for _ in tensor.shape)]

        block = ctx.enter_context(nc.Block())

        @block.sync
        def _(sp):
            for s in signals:
                sp.sem_inc(s.sem, s.per)
            for i in range(4):
                n = TILES // 4
                sp.dma_start(x[:, i * n:(i + 1) * n, :], a["x"][:, i * n:(i + 1) * n, :]).then_inc(s_x, 16)
            for dst, src in CONSTS:
                sp.dma_start(full(dst), src).then_inc(s_const, 16)
            sp.dma_start(w_in[:, F:2 * F], a["w1"]).then_inc(s_const, 16)
            sp.dma_start(bg[:, :], a["bg"].to_broadcast([P, 1])).then_inc(s_const, 16)
            for i in range(5):
                if i >= 2:
                    sp.wait_ge(w_split, 2 * (i - 1))
                sp.dma_start(stage[:, i % 2, :], a["w_attn"][i]).then_inc(s_w[i % 2], 16)
            with sp.Fori(0, B // WIDE) as t:
                sp.wait_ge(L4["x"].sem, L4["x"].nth(t, WIDE))
                sp.dma_start(out[:, bass.ds(t * (WIDE * NT), WIDE * NT), :],
                             x[:, bass.ds(t * (WIDE * NT), WIDE * NT), :]).then_inc(s_out, 16)
            sp.wait_ge(s_out, 16 * (B // WIDE))

        N_CONST = 16 * (len(CONSTS) + 2)

        def row_tiles(t):
            return x[:, bass.ds(t * NT, NT), :]

        @block.vector
        def _(dve):
            dve.memset(ones_row[:, :], 1.0).then_inc(pre_v, 1)
            dve.memset(val1[:, :, :, DH:DH + 1], 1.0).then_inc(pre_v, 1)
            dve.wait_ge(s_const, N_CONST)
            dve.tensor_copy(ident_bf[:, :], ident[:, :]).then_inc(pre_v, 1)
            dve.tensor_copy(causal_bf[:, :], causal[:, :]).then_inc(pre_v, 1)
            dve.tensor_copy(first_bf[:, :], first[:, :]).then_inc(pre_v, 1)
            dve.wait_ge(pre_s, 1)
            dve.tensor_tensor(silu[:, :, :], cT[:, :, :], silu_e[:, :, :], ALU.mult).then_inc(pre_v, 1)
            dve.wait_ge(pre_t, 1)
            for l in range(2):
                for k in range(4):
                    dve.tensor_scalar(modT[:, l, k, :], bank[0][:, (l * 4 + k) * B:(l * 4 + k + 1) * B],
                                      float(k % 2), None, ALU.add).then_inc(pre_v, 1)
            raw = bank[1][0:B, :].rearrange("b (l k d) -> b l k d", l=2, k=2)
            dve.tensor_copy(gate_row[:, :, :, :], raw).then_inc(pre_v, 1)
            dve.wait_ge(pre_v, 15)
            dve.tensor_scalar(gate_hi[:, :, :, :], gate_row[:, :, :, :], 0.25, None, ALU.max).then_inc(pre_v, 1)
            dve.tensor_scalar(gate_lo[:, :, :, :], gate_row[:, :, :, :], -0.25, None, ALU.min).then_inc(pre_v, 1)
            dve.wait_ge(pre_v, 17)

            def flat(t):
                return t[:, :, :, :].rearrange("b l k d -> b (l k d)")

            dve.scalar_tensor_tensor(out=flat(gate_a), in0=flat(gate_row), scalar=0.0, in1=flat(gate_hi),
                                     op0=ALU.is_ge, op1=ALU.mult).then_inc(pre_v, 1)
            dve.scalar_tensor_tensor(out=flat(gate_b), in0=flat(gate_row), scalar=0.0, in1=flat(gate_lo),
                                     op0=ALU.is_lt, op1=ALU.mult).then_inc(pre_v, 1)
            dve.wait_ge(pre_v, 19)
            dve.tensor_tensor(flat(gate_row), flat(gate_a), flat(gate_b), ALU.add).then_inc(pre_v, 1)
            dve.wait_ge(pre_t, 2)
            dve.tensor_copy(w_in[:, 0:F], bank[2][:, :]).then_inc(pre_v, 1)
            dve.tensor_copy(uv1[:, :], bank[3][:, :]).then_inc(pre_v, 1)
            dve.tensor_copy(uv2[:, :, :], bank[4][:, :].rearrange("p (c d) -> p c d", c=FC)).then_inc(pre_v, 1)
            dve.wait_ge(pre_v, 23)
            dve.tensor_copy(w_in_hi[:, :], w_in[:, :]).then_inc(pre_v, 1)
            dve.wait_ge(pre_v, 24)
            dve.tensor_tensor(w_in_lo[:, :], w_in[:, :], w_in_hi[:, :].bitcast(F32), ALU.subtract).then_inc(pre_v, 1)
            for i in range(5):
                dve.wait_ge(s_w[i % 2], 16 * (i // 2 + 1))
                dve.tensor_copy(w_hi[:, i, :], stage[:, i % 2, :]).then_inc(w_split, 1)
                dve.wait_ge(w_split, 2 * i + 1)
                dve.tensor_tensor(w_lo[:, i, :], stage[:, i % 2, :], w_hi[:, i, :].bitcast(F32),
                                  ALU.subtract).then_inc(w_split, 1)
            dve.wait_ge(s_x, 64)
            for i in range(TILES):
                dve.bn_stats(stats[:, i, :], x[:, i, :]).then_inc(pre_v, 1)
            dve.wait_ge(pre_v, 25 + TILES)

            def finish_rstd(n):
                done = [ROOT_STEPS * n]

                def then(ins, wait=True):
                    ins.then_inc(st_v, 1)
                    done[0] += 1
                    if wait:
                        dve.wait_ge(st_v, done[0])

                then(dve.tensor_tensor(apart[:, :], stats[:, :, 1], stats[:, :, 4], ALU.subtract), False)
                then(dve.tensor_tensor(mean[:, :], stats[:, :, 1], stats[:, :, 4], ALU.add), False)
                then(dve.tensor_tensor(var[:, :], stats[:, :, 2], stats[:, :, 5], ALU.add))
                then(dve.scalar_tensor_tensor(out=apart[:, :], in0=apart[:, :], scalar=0.25, in1=apart[:, :],
                                              op0=ALU.mult, op1=ALU.mult), False)
                then(dve.tensor_scalar(var[:, :], var[:, :], 1.0 / D, EPS, ALU.mult, ALU.add))
                then(dve.tensor_scalar(mean[:, :], mean[:, :], 0.5, None, ALU.mult), False)
                then(dve.tensor_tensor(var[:, :], var[:, :], apart[:, :], ALU.add))
                dve.wait_ge(st_s, n + 1)
                then(dve.reciprocal(rstd[:, :], root[:, :]))
                then(dve.tensor_tensor(newton[:, :], var[:, :], rstd[:, :], ALU.mult))
                then(dve.tensor_tensor(newton[:, :], newton[:, :], rstd[:, :], ALU.mult))
                then(dve.tensor_scalar(newton[:, :], newton[:, :], -0.5, 1.5, ALU.mult, ALU.add))
                then(dve.tensor_tensor(rstd[:, :], rstd[:, :], newton[:, :], ALU.mult))
                assert done[0] == ROOT_STEPS * (n + 1)

            def normalise(S, t, w, row, nth):
                dve.wait_ge(S["xT"].sem, S["xT"].before(t, nth))
                for j in range(NT):
                    i = row * NT + j
                    last = dve.tensor_scalar(
                        xn[:, w, j, :], x[:, bass.ds(i, 1), :].rearrange("p o d -> p (o d)"),
                        mean[:, bass.ds(i, 1)], rstd[:, bass.ds(i, 1)], ALU.subtract, ALU.mult)
                last.then_inc(S["xn"].sem, 1)

            def add_gated(S, t, w, row, nth, psum, l, k, with_stats=True):
                dve.wait_ge(S["y"].sem, S["y"].nth(t, nth))
                gate_bc = gate[:, l, k, bass.ds(row, 1), :].to_broadcast([P, NT, D])
                dve.tensor_tensor(step[:, w, :, :], psum, gate_bc, ALU.mult).then_inc(S["gated"].sem, 1)
                dve.wait_ge(S["gated"].sem, S["gated"].nth(t, nth))
                dve.tensor_tensor(row_tiles(row), row_tiles(row), step[:, w, :, :], ALU.add).then_inc(S["x"].sem, 1)
                if not with_stats:
                    return
                dve.wait_ge(S["x"].sem, S["x"].nth(t, nth))
                for j in range(NT):
                    i = row * NT + j
                    last = dve.bn_stats(stats[:, bass.ds(i, 1), :].rearrange("p o s -> p (o s)"),
                                        x[:, bass.ds(i, 1), :].rearrange("p o d -> p (o d)"))
                last.then_inc(S["stats"].sem, 1)

            def as_tiles(ps):
                return ps.rearrange("p (j d) -> p j d", j=NT)

            finish_rstd(0)
            with dve.Fori(0, B // WIDE) as t:
                for w in range(WIDE):
                    normalise(L1, t, w, t * WIDE + w, w + 1)
                for w in range(WIDE):
                    dve.wait_ge(L1["g"].sem, L1["g"].nth(t, w + 1))
                    dve.wait_ge(L1["scanned"].sem, L1["scanned"].before(t, w + 1))
                    dve.tensor_scalar(keep[:, w, :], g[:, w, :], -1.0, 1.0, ALU.mult, ALU.add)\
                       .then_inc(L1["keep"].sem, 1)
                    dve.tensor_tensor(gh[:, w, :], g[:, w, :], hT[:, w, :], ALU.mult).then_inc(L1["gh"].sem, 1)
                    dve.wait_ge(L1["keep"].sem, L1["keep"].nth(t, w + 1))
                    dve.wait_ge(L1["gh"].sem, L1["gh"].nth(t, w + 1))
                    dve.tensor_tensor_scan(scanned[:, w, :], keep[:, w, :], gh[:, w, :], 0.0,
                                           ALU.mult, ALU.add).then_inc(L1["scanned"].sem, 1)
                for w in range(WIDE):
                    add_gated(L1, t, w, t * WIDE + w, w + 1, as_tiles(bank[2 * w][:, 0:T]), 0, 0)
            dve.wait_ge(L1["stats"].sem, L1["stats"].nth(B // WIDE - 1, WIDE))

            def split_h(S, t):
                dve.wait_ge(S["h"].sem, S["h"].nth(t, 1))
                dve.tensor_copy(h_hi[:, :], hT[:, 0, :]).then_inc(S["hi"].sem, 1)
                dve.wait_ge(S["hi"].sem, S["hi"].nth(t, 1))
                dve.tensor_tensor(h_lo[:, :], hT[:, 0, :], h_hi[:, :].bitcast(F32), ALU.subtract)\
                   .then_inc(S["lo"].sem, 1)

            finish_rstd(1)
            with dve.Fori(0, B) as t:
                normalise(L2, t, 0, t, 1)
                split_h(L2, t)
                for j in range(NT):
                    groups = bank[1 + j][:, :].rearrange("p (g k) -> p g k", g=GROUPS)
                    dve.wait_ge(L2["logits"].sem, L2["logits"].nth(t, j + 1))
                    dve.tensor_reduce(top[:, j, :], groups, AX_X, ALU.max).then_inc(L2["top"].sem, 1)
                    dve.wait_ge(L2["top"].sem, L2["top"].nth(t, j + 1))
                    dve.tensor_tensor(hits[:, j, :].rearrange("p (g k) -> p g k", g=GROUPS), groups,
                                      top[:, j, :].unsqueeze(2).to_broadcast([P, GROUPS, PICK]),
                                      ALU.is_ge).then_inc(L2["hits"].sem, 1)
                for c2 in range(2):
                    dve.wait_ge(L2["hidden"].sem, L2["hidden"].nth(t, 1))
                    dve.wait_ge(L2["picked"].sem, L2["picked"].nth(t, c2 + 1))
                    dve.scalar_tensor_tensor(
                        out=hid[:, 0, 2 * c2:2 * c2 + 2, :].rearrange("p c t -> p (c t)"),
                        in0=bank[6 + c2][:, :], scalar=0.0,
                        in1=picked[:, 2 * c2:2 * c2 + 2, :].rearrange("p c t -> p (c t)"),
                        op0=ALU.max, op1=ALU.mult).then_inc(L2["hid"].sem, 1)
                add_gated(L2, t, 0, t, 1, as_tiles(bank[0][:, 0:T]), 0, 1)
            dve.wait_ge(L2["stats"].sem, L2["stats"].nth(B - 1, 1))

            finish_rstd(2)
            with dve.Fori(0, B) as t:
                normalise(L3, t, 0, t, 1)
                split_h(L3, t)
                for u in range(4):
                    rest = val_rest[:, u // 2, (u % 2) * 512:(u % 2 + 1) * 512]
                    dve.wait_ge(L3["v1"].sem, L3["v1"].nth(t, u + 1))
                    heads = slice((u % 2) * 8, (u % 2) * 8 + 8)
                    dve.tensor_tensor(rest.rearrange("p (h d) -> p h d", h=8),
                                      bank[u % 2][:, :].rearrange("p (h d) -> p h d", h=8),
                                      val1[:, u // 2, heads, 0:DH], ALU.subtract).then_inc(L3["rest"].sem, 1)

                def rotate(p):
                    dve.wait_ge(L3["qk_ps"].sem, L3["qk_ps"].nth(t, p + 1))
                    if p >= 2:
                        dve.wait_ge(L3["rope"].sem, L3["rope"].nth(t, p - 1))
                    dve.tensor_tensor(rope_a[:, p % 2, :], bank[0][:, :],
                                      rope_tab[:, 0:2, :].rearrange("p a t -> p (a t)"), ALU.mult)
                    dve.tensor_tensor(rope_b[:, p % 2, :], bank[1][:, :],
                                      rope_tab[:, 2:4, :].rearrange("p a t -> p (a t)"), ALU.mult)\
                       .then_inc(L3["mul"].sem, 1)

                def row_max(h):
                    s = bank[2 + h % 2]
                    dve.wait_ge(L3["s"].sem, L3["s"].nth(t, h + 1))
                    dve.tensor_reduce(nmax[:, h % 4, 0:1], s[:, 0:P], AX_X, ALU.max, negate=True)
                    dve.tensor_reduce(nmax[:, h % 4, 1:2], s[:, P:3 * P], AX_X, ALU.max, negate=True)\
                       .then_inc(L3["nmax"].sem, 1)

                def low_part(h):
                    dve.wait_ge(L3["pT_hi"].sem, L3["pT_hi"].nth(t, h + 1))
                    dve.scalar_tensor_tensor(out=probsT_lo[:, h % 4, :], in0=bank[4 + h % 2][:, 0:3 * P],
                                             scalar=P_SCALE, in1=probsT_hi[:, h % 4, :],
                                             op0=ALU.mult, op1=ALU.subtract).then_inc(L3["pT_lo"].sem, 1)

                def divide(p):
                    ov = bank[6][:, 0:4 * (DH + 1)].rearrange("p (q d) -> p q d", q=4)
                    dve.wait_ge(L3["pv"].sem, L3["pv"].nth(t, p + 1))
                    dve.reciprocal(rsum[:, p % 2, :], ov[:, :, DH]).then_inc(L3["rsum"].sem, 1)
                    dve.wait_ge(L3["rsum"].sem, L3["rsum"].nth(t, p + 1))
                    if p >= 2:
                        dve.wait_ge(L3["oT_ps"].sem, L3["oT_ps"].nth(t, p - 1))
                    dve.tensor_tensor(o[:, p % 2, :, :, :].rearrange("p j h d -> p (j h) d"), ov[:, :, 0:DH],
                                      rsum[:, p % 2, :].unsqueeze(2).to_broadcast([P, 4, DH]), ALU.mult)\
                       .then_inc(L3["o"].sem, 1)

                rotate(0)
                rotate(1)
                for p in range(PAIRS):
                    if p >= 1:
                        low_part(2 * p - 2)
                        low_part(2 * p - 1)
                    row_max(2 * p)
                    row_max(2 * p + 1)
                    if p + 2 < PAIRS:
                        rotate(p + 2)
                    if p >= 1:
                        divide(p - 1)
                low_part(H - 2)
                low_part(H - 1)
                divide(PAIRS - 1)
                add_gated(L3, t, 0, t, 1, as_tiles(bank[0][:, 0:T]), 1, 0)
            dve.wait_ge(L3["stats"].sem, L3["stats"].nth(B - 1, 1))

            finish_rstd(3)
            with dve.Fori(0, B // WIDE) as t:
                for w in range(WIDE):
                    normalise(L4, t, w, t * WIDE + w, w + 1)
                for w in range(WIDE):
                    add_gated(L4, t, w, t * WIDE + w, w + 1, as_tiles(bank[4 + w][:, 0:T]), 1, 1, with_stats=False)

        @block.scalar
        def _(act):
            act.wait_ge(s_const, N_CONST)
            act.activation(silu_e[:, :, :], cT[:, :, :], ACT.Sigmoid).then_inc(pre_s, 1)
            for n in range(B):
                l, k, q = n // 8, n // 4 % 2, n % 4
                act.wait_ge(pre_t, 3 + n)
                act.activation(gate[:, l, k, 4 * q:4 * q + 4, :],
                               bank[n % 8][:, :].rearrange("p (r d) -> p r d", r=4), ACT.Copy).then_inc(pre_s, 1)

            def roots(n):
                act.wait_ge(st_v, ROOT_STEPS * n + 7)
                act.activation(root[:, :], var[:, :], ACT.Sqrt).then_inc(st_s, 1)

            def modulate(S, t, w, row, nth, psum, l, k):
                act.wait_ge(S["xT"].sem, S["xT"].nth(t, nth))
                act.activation(hT[:, w, :], psum, ACT.Identity, bias=modT[:, l, 2 * k, bass.ds(row, 1)],
                               scale=modT[:, l, 2 * k + 1, bass.ds(row, 1)]).then_inc(S["h"].sem, 1)

            roots(0)
            with act.Fori(0, B // WIDE) as t:
                for w in range(WIDE):
                    act.wait_ge(L1["gh"].sem, L1["gh"].before(t, w + 1))
                    modulate(L1, t, w, t * WIDE + w, w + 1, bank[2 * w][:, 0:T], 0, 0)
                for w in range(WIDE):
                    act.wait_ge(L1["z"].sem, L1["z"].nth(t, w + 1))
                    act.activation(g[:, w, :], bank[2 * w + 1][:, 0:T], ACT.Sigmoid, bias=bg[:, 0:1])\
                       .then_inc(L1["g"].sem, 1)
            roots(1)
            with act.Fori(0, B) as t:
                act.wait_ge(L2["lo"].sem, L2["lo"].before(t, 1))
                modulate(L2, t, 0, t, 1, bank[0][:, 0:T], 0, 1)
                act.wait_ge(L2["hitsT_ps"].sem, L2["hitsT_ps"].nth(t, 1))
                act.activation(hitsT[:, :, :].rearrange("p c t -> p (c t)"), bank[3][:, :].bitcast(BF16), ACT.Copy)\
                   .then_inc(L2["hitsT"].sem, 1)
                act.wait_ge(L2["first"].sem, L2["first"].nth(t, 1))
                for c2 in range(2):
                    act.activation(picked[:, 2 * c2:2 * c2 + 2, :].rearrange("p c t -> p (c t)"),
                                   bank[4 + c2][:, :], ACT.Relu).then_inc(L2["picked"].sem, 1)
            roots(2)
            with act.Fori(0, B) as t:
                act.wait_ge(L3["lo"].sem, L3["lo"].before(t, 1))
                modulate(L3, t, 0, t, 1, bank[0][:, 0:T], 1, 0)
                for u in range(4):
                    heads = slice((u % 2) * 8, (u % 2) * 8 + 8)
                    act.wait_ge(L3["v_ps"].sem, L3["v_ps"].nth(t, u + 1))
                    act.activation(val1[:, u // 2, heads, 0:DH],
                                   bank[u % 2][:, :].rearrange("p (h d) -> p h d", h=8), ACT.Copy)\
                       .then_inc(L3["v1"].sem, 1)
                for u in range(4):
                    heads = slice((u % 2) * 8, (u % 2) * 8 + 8)
                    act.wait_ge(L3["rest"].sem, L3["rest"].nth(t, u + 1))
                    act.activation(val2[:, u // 2, heads, :],
                                   val_rest[:, u // 2, (u % 2) * 512:(u % 2 + 1) * 512]
                                   .rearrange("p (h d) -> p h d", h=8), ACT.Copy).then_inc(L3["v2"].sem, 1)

                def high_part(h):
                    act.wait_ge(L3["pT"].sem, L3["pT"].nth(t, h + 1))
                    if h >= 4:
                        act.wait_ge(L3["pv"].sem, L3["pv"].nth(t, h // 2 - 1))
                    act.activation(probsT_hi[:, h % 4, :], bank[4 + h % 2][:, 0:3 * P], ACT.Copy,
                                   scale=P_SCALE).then_inc(L3["pT_hi"].sem, 1)

                def exps(h):
                    s = bank[2 + h % 2]
                    act.wait_ge(L3["nmax"].sem, L3["nmax"].nth(t, h + 1))
                    if h >= 4:
                        act.wait_ge(L3["pT"].sem, L3["pT"].nth(t, h - 3))
                    act.activation(probs[:, h % 4, 0:P], s[:, 0:P], ACT.Exp, bias=nmax[:, h % 4, 0:1])
                    act.activation(probs[:, h % 4, P:3 * P], s[:, P:3 * P], ACT.Exp, bias=nmax[:, h % 4, 1:2])\
                       .then_inc(L3["exp"].sem, 1)

                def heads_out(p):
                    act.wait_ge(L3["oT_ps"].sem, L3["oT_ps"].nth(t, p + 1))
                    act.activation(oT[:, p, :], bank[7][:, (p % 2) * T:(p % 2 + 1) * T], ACT.Copy)\
                       .then_inc(L3["oT"].sem, 1)

                for p in range(PAIRS):
                    if p >= 1:
                        high_part(2 * p - 2)
                        high_part(2 * p - 1)
                    exps(2 * p)
                    exps(2 * p + 1)
                    if p >= 2:
                        heads_out(p - 2)
                high_part(H - 2)
                high_part(H - 1)
                heads_out(PAIRS - 2)
                heads_out(PAIRS - 1)
            roots(3)
            with act.Fori(0, B // WIDE) as t:
                for w in range(WIDE):
                    act.wait_ge(L4["up"].sem, L4["up"].before(t, w + 1))
                    modulate(L4, t, w, t * WIDE + w, w + 1, bank[4 + w][:, 0:T], 1, 1)
                for w in range(WIDE):
                    for c in range(FC):
                        act.wait_ge(L4["up"].sem, L4["up"].nth(t, w + 1))
                        act.wait_ge(L4["y"].sem, L4["y"].before(t, w + 1))
                        act.activation(hid[:, w, c, :], bank[2 * (w % 2) + c // 2][:, (c % 2) * T:(c % 2 + 1) * T],
                                       ACT.Gelu_apprx_tanh, bias=b1[:, c:c + 1]).then_inc(L4["act"].sem, 1)

        @block.gpsimd
        def _(pool):
            with pool.Fori(0, B) as t:
                for u in range(4):
                    part = (slice(None), u // 2, slice((u % 2) * 8, (u % 2) * 8 + 8), slice(None))
                    pool.wait_ge(L3["v2"].sem, L3["v2"].nth(t, u + 1))
                    pool.tensor_tensor(val3[part],
                                       val_rest[:, u // 2, (u % 2) * 512:(u % 2 + 1) * 512]
                                       .rearrange("p (h d) -> p h d", h=8), val2[part], ALU.subtract)\
                        .then_inc(L3["v3"].sem, 1)
                for p in range(PAIRS):
                    pool.wait_ge(L3["mul"].sem, L3["mul"].nth(t, p + 1))
                    if p >= 4:
                        pool.wait_ge(L3["s"].sem, L3["s"].nth(t, 2 * (p - 4) + 2))
                    pool.tensor_tensor(qk[:, p % 4, :, :].rearrange("p a t -> p (a t)"), rope_a[:, p % 2, :],
                                       rope_b[:, p % 2, :], ALU.add).then_inc(L3["rope"].sem, 1)

        @block.tensor
        def _(pe):
            pe.wait_ge(pre_v, 6)
            for l in range(2):
                for k, part in enumerate((0, 1, 3, 4)):
                    pe.matmul(bank[0][:, (l * 4 + k) * B:(l * 4 + k + 1) * B],
                              wmod[:, l, part * D:(part + 1) * D], silu[:, l, :], start=True, stop=True)
                for k, part in enumerate((2, 5)):
                    last = pe.matmul(bank[1][0:B, (l * 2 + k) * D:(l * 2 + k + 1) * D], silu[:, l, :],
                                     wmod[:, l, part * D:(part + 1) * D], start=True, stop=True)
            last.then_inc(pre_t, 1)
            pe.matmul(bank[2][:, :], m1T[:, :], m2[:, :], start=True, stop=True)
            pe.matmul(bank[3][:, :], u1T[:, :], v1[:, :], start=True, stop=True)
            for c in range(FC):
                last = pe.matmul(bank[4][:, c * D:(c + 1) * D], u2T[:, c * P:(c + 1) * P], v2[:, :],
                                 start=True, stop=True)
            last.then_inc(pre_t, 1)
            pe.wait_ge(pre_v, 23)
            for n in range(B):
                l, k, q = n // 8, n // 4 % 2, n % 4
                if n >= 8:
                    pe.wait_ge(pre_s, 1 + n - 7)
                for r in range(4):
                    last = pe.matmul(bank[n % 8][:, r * D:(r + 1) * D],
                                     ident[0:B, 4 * q + r:4 * q + r + 1].to_broadcast([B, P]),
                                     gate_row[:, l, k, :], start=True, stop=True)
                last.then_inc(pre_t, 1)

            def to_d_major(S, t, w, nth, psum):
                pe.wait_ge(S["xn"].sem, S["xn"].nth(t, nth))
                for j in range(NT):
                    last = pe.transpose(psum[:, j * P:(j + 1) * P], xn[:, w, j, :], ident[:, :])
                last.then_inc(S["xT"].sem, 1)

            def bias(psum, k, start, stop=True):
                return pe.matmul(psum, ones_row[:, :], bias_rows[:, k, :], start=start, stop=stop)

            pe.wait_ge(pre_s, 1 + B)
            with pe.Fori(0, B // WIDE) as t:
                for w in range(WIDE):
                    pe.wait_ge(L1["gated"].sem, L1["gated"].before(t, w + 1))
                    to_d_major(L1, t, w, w + 1, bank[2 * w])
                for w in range(WIDE):
                    pe.wait_ge(L1["h"].sem, L1["h"].nth(t, w + 1))
                    pe.wait_ge(L1["g"].sem, L1["g"].before(t, w + 1))
                    pe.matmul(bank[2 * w + 1][:, 0:T], wg[:, 0:1].to_broadcast([P, P]), hT[:, w, :],
                              start=True, stop=True).then_inc(L1["z"].sem, 1)
                for w in range(WIDE):
                    pe.wait_ge(L1["scanned"].sem, L1["scanned"].nth(t, w + 1))
                    for j in range(NT):
                        ps = bank[2 * w][:, j * P:(j + 1) * P]
                        pe.matmul(ps, scanned[:, w, j * P:(j + 1) * P], woutT[:, :], start=True, stop=False)
                        last = bias(ps, 0, False)
                    last.then_inc(L1["y"].sem, 1)

            with pe.Fori(0, B) as t:
                pe.wait_ge(L2["gated"].sem, L2["gated"].before(t, 1))
                to_d_major(L2, t, 0, 1, bank[0])
                pe.wait_ge(L2["lo"].sem, L2["lo"].nth(t, 1))
                for j in range(NT):
                    tok = slice(j * P, (j + 1) * P)
                    ps = bank[1 + j][:, :]
                    pe.wait_ge(L2["hits"].sem, L2["hits"].before(t, j + 1))
                    pe.matmul(ps, h_hi[:, tok], w_in_hi[:, 0:F], start=True, stop=False)
                    pe.matmul(ps, h_hi[:, tok], w_in_lo[:, 0:F], start=False, stop=False)
                    pe.matmul(ps, h_lo[:, tok], w_in_hi[:, 0:F], start=False, stop=False)
                    pe.matmul(ps, ones_row[:, :], mb_row[:, :], start=False, stop=True)\
                      .then_inc(L2["logits"].sem, 1)
                pe.wait_ge(L2["hid"].sem, L2["hid"].before(t, 2))
                for c in range(FC):
                    f = slice(F + c * P, F + (c + 1) * P)
                    ps = bank[6 + c // 2][:, (c % 2) * T:(c % 2 + 1) * T]
                    pe.matmul(ps, w_in_hi[:, f], h_hi[:, :], start=True, stop=False)
                    pe.matmul(ps, w_in_hi[:, f], h_lo[:, :], start=False, stop=False)
                    last = pe.matmul(ps, w_in_lo[:, f], h_hi[:, :], start=False, stop=True)
                last.then_inc(L2["hidden"].sem, 1)
                hits_ps = bank[3][:, :].bitcast(BF16)
                for j in range(NT):
                    pe.wait_ge(L2["hits"].sem, L2["hits"].nth(t, j + 1))
                    for c in range(FC):
                        last = pe.transpose(hits_ps[:, c * T + j * P:c * T + (j + 1) * P],
                                            hits[:, j, c * P:(c + 1) * P], ident_bf[:, :])
                last.then_inc(L2["hitsT_ps"].sem, 1)
                pe.wait_ge(L2["hitsT"].sem, L2["hitsT"].nth(t, 1))
                for c in range(FC):
                    last = pe.matmul(bank[4 + c // 2][:, (c % 2) * T:(c % 2 + 1) * T], first_bf[:, :],
                                     hitsT[:, c, :], start=True, stop=True)
                last.then_inc(L2["first"].sem, 1)
                pe.wait_ge(L2["hid"].sem, L2["hid"].nth(t, 2))
                for j in range(NT):
                    ps = bank[0][:, j * P:(j + 1) * P]
                    for c in range(FC):
                        pe.matmul(ps, hid[:, 0, c, j * P:(j + 1) * P], w2[:, c, :], start=(c == 0), stop=False)
                    last = bias(ps, 1, False)
                last.then_inc(L2["y"].sem, 1)

            with pe.Fori(0, B) as t:
                pe.wait_ge(L3["gated"].sem, L3["gated"].before(t, 1))
                to_d_major(L3, t, 0, 1, bank[0])
                pe.wait_ge(L3["lo"].sem, L3["lo"].nth(t, 1))
                for u in range(4):
                    tok = slice(u // 2 * P, (u // 2 + 1) * P)
                    cols = slice((u % 2) * 512, (u % 2 + 1) * 512)
                    if u >= 2:
                        pe.wait_ge(L3["rest"].sem, L3["rest"].nth(t, u - 1))
                    ps = bank[u % 2][:, :]
                    pe.matmul(ps, h_hi[:, tok], w_hi[:, 4, cols], start=True, stop=False)
                    pe.matmul(ps, h_hi[:, tok], w_lo[:, 4, cols], start=False, stop=False)
                    pe.matmul(ps, h_lo[:, tok], w_hi[:, 4, cols], start=False, stop=True)\
                      .then_inc(L3["v_ps"].sem, 1)

                def project(p):
                    if p == 0:
                        pe.wait_ge(L3["rest"].sem, L3["rest"].nth(t, 4))
                    else:
                        pe.wait_ge(L3["mul"].sem, L3["mul"].nth(t, p))
                    cols = slice(p * P, (p + 1) * P)
                    for i, (b, half) in enumerate(((0, 0), (1, 0), (0, 1), (1, 1))):
                        ps = bank[b][:, half * T:(half + 1) * T]
                        pe.matmul(ps, w_hi[:, i, cols], h_hi[:, :], start=True, stop=False)
                        pe.matmul(ps, w_hi[:, i, cols], h_lo[:, :], start=False, stop=False)
                        last = pe.matmul(ps, w_lo[:, i, cols], h_hi[:, :], start=False, stop=True)
                    last.then_inc(L3["qk_ps"].sem, 1)

                def scores(h):
                    p, rows = h // 2, slice((h % 2) * DH, (h % 2 + 1) * DH)
                    pe.wait_ge(L3["rope"].sem, L3["rope"].nth(t, p + 1))
                    if h >= 2:
                        pe.wait_ge(L3["exp"].sem, L3["exp"].nth(t, h - 1))
                    s = bank[2 + h % 2]
                    q, k = qk[rows, p % 4, 0, :], qk[rows, p % 4, 1, :]
                    pe.matmul(s[:, 0:P], q[:, 0:P], k[:, 0:P], start=True, stop=False)
                    pe.matmul(s[:, 0:P], ident_bf[:, :], causal_bf[:, :], start=False, stop=True)
                    pe.matmul(s[:, P:3 * P], q[:, P:T], k[:, :], start=True, stop=False)
                    pe.matmul(s[:, 2 * P:3 * P], ident_bf[:, :], causal_bf[:, :], start=False, stop=True)\
                      .then_inc(L3["s"].sem, 1)

                def transpose_probs(h):
                    pe.wait_ge(L3["exp"].sem, L3["exp"].nth(t, h + 1))
                    if h >= 2:
                        pe.wait_ge(L3["pT_lo"].sem, L3["pT_lo"].nth(t, h - 1))
                    for blk in range(3):
                        cols = slice(blk * P, (blk + 1) * P)
                        last = pe.transpose(bank[4 + h % 2][:, cols], probs[:, h % 4, cols], ident[:, :])
                    last.then_inc(L3["pT"].sem, 1)

                def weigh(h):
                    p = h // 2
                    pe.wait_ge(L3["pT_lo"].sem, L3["pT_lo"].nth(t, h + 1))
                    if h == 0:
                        pe.wait_ge(L3["v3"].sem, L3["v3"].nth(t, 4))
                    if h % 2 == 0 and p >= 1:
                        pe.wait_ge(L3["o"].sem, L3["o"].nth(t, p))
                    for j in range(NT):
                        at = (2 * j + h % 2) * (DH + 1)
                        wide = bank[6][:, at:at + DH + 1]
                        thin = bank[6][:, at:at + DH]
                        for kt in range(j + 1):
                            blk = slice((j + kt) * P, (j + kt + 1) * P)
                            hi, lo = probsT_hi[:, h % 4, blk], probsT_lo[:, h % 4, blk]
                            pe.matmul(wide, hi, val1[:, kt, h, :], start=(kt == 0), stop=False)
                            pe.matmul(thin, hi, val2[:, kt, h, :], start=False, stop=False)
                            pe.matmul(thin, hi, val3[:, kt, h, :], start=False, stop=False)
                            pe.matmul(wide, lo, val1[:, kt, h, :], start=False, stop=False)
                            last = pe.matmul(thin, lo, val2[:, kt, h, :], start=False, stop=(kt == j))
                    if h % 2 == 1:
                        last.then_inc(L3["pv"].sem, 1)

                def heads_to_rows(p):
                    pe.wait_ge(L3["o"].sem, L3["o"].nth(t, p + 1))
                    if p >= 1:
                        pe.wait_ge(L3["oT"].sem, L3["oT"].nth(t, p))
                    for j in range(NT):
                        at = (p % 2) * T + j * P
                        last = pe.transpose(bank[7][:, at:at + P],
                                            o[:, p % 2, j, :, :].rearrange("p h d -> p (h d)"), ident[:, :])
                    last.then_inc(L3["oT_ps"].sem, 1)

                project(0)
                project(1)
                for p in range(PAIRS):
                    if p >= 1:
                        transpose_probs(2 * p - 2)
                        transpose_probs(2 * p - 1)
                    scores(2 * p)
                    scores(2 * p + 1)
                    if p + 2 < PAIRS:
                        project(p + 2)
                    if p >= 1:
                        weigh(2 * p - 2)
                        weigh(2 * p - 1)
                    if p >= 2:
                        heads_to_rows(p - 2)
                transpose_probs(H - 2)
                transpose_probs(H - 1)
                weigh(H - 2)
                weigh(H - 1)
                heads_to_rows(PAIRS - 2)
                heads_to_rows(PAIRS - 1)
                pe.wait_ge(L3["mul"].sem, L3["mul"].nth(t, PAIRS))
                pe.wait_ge(L3["oT"].sem, L3["oT"].nth(t, PAIRS))
                for j in range(NT):
                    for p in range(PAIRS):
                        last = pe.matmul(bank[0][:, j * P:(j + 1) * P], oT[:, p, j * P:(j + 1) * P], woT[:, p, :],
                                         start=(p == 0), stop=(p == PAIRS - 1))
                last.then_inc(L3["y"].sem, 1)

            pe.wait_ge(L3["gated"].sem, L3["gated"].nth(B - 1, 1))
            with pe.Fori(0, B // WIDE) as t:
                for w in range(WIDE):
                    pe.wait_ge(L4["gated"].sem, L4["gated"].before(t, w + 1))
                    to_d_major(L4, t, w, w + 1, bank[4 + w])
                for w in range(WIDE):
                    pe.wait_ge(L4["h"].sem, L4["h"].nth(t, w + 1))
                    if w >= 2:
                        pe.wait_ge(L4["act"].sem, L4["act"].nth(t, FC * (w - 1)))
                    else:
                        pe.wait_ge(L4["act"].sem, L4["act"].before(t, FC * (w + 3)))
                    for c in range(FC):
                        last = pe.matmul(bank[2 * (w % 2) + c // 2][:, (c % 2) * T:(c % 2 + 1) * T],
                                         uv1[:, c * P:(c + 1) * P], hT[:, w, :], start=True, stop=True)
                    last.then_inc(L4["up"].sem, 1)
                for w in range(WIDE):
                    pe.wait_ge(L4["act"].sem, L4["act"].nth(t, FC * (w + 1)))
                    for j in range(NT):
                        ps = bank[4 + w][:, j * P:(j + 1) * P]
                        for c in range(FC):
                            pe.matmul(ps, hid[:, w, c, j * P:(j + 1) * P], uv2[:, c, :], start=(c == 0), stop=False)
                        last = bias(ps, 2, False)
                    last.then_inc(L4["y"].sem, 1)


def constants():
    inv_freq = (1.0 / np.float32(10000.0) ** (np.arange(0, DH, 2, dtype=np.float32) / np.float32(DH))).astype(np.float32)
    angle = np.outer(np.arange(T, dtype=np.float32), inv_freq).astype(np.float32)
    cos, sin = np.cos(angle).T, np.sin(angle).T
    cos4 = np.concatenate([cos] * 4)
    sin4 = np.concatenate([-sin, sin] * 2)
    scale = np.float32(DH ** -0.5)
    rope = np.stack([cos4 * scale, cos4, sin4 * scale, sin4], axis=1).astype(np.float32)
    i = np.arange(P)
    causal = np.where(i[None, :] > i[:, None], np.float32(-1e30), np.float32(0))
    same = (i[:, None] // PICK == i[None, :] // PICK) & (i[:, None] < i[None, :])
    first = np.eye(P, dtype=np.float32) - 2 * same.astype(np.float32)
    return {"ident": np.eye(P, dtype=np.float32), "causal": causal.astype(np.float32), "first": first, "rope": rope}


def kernel(**inputs):
    import numpy as _np
    import concourse.bacc as _bacc
    from concourse import mybir as _mybir
    from concourse.bass_utils import run_bass_kernel_spmd as _run

    i = {k: _np.asarray(v) for k, v in inputs.items()}

    def swapped(w):
        return w.reshape(H, 2, HALF, D)[:, ::-1].reshape(H * DH, D)

    wq, wk, wv = i["L1_attn_wq"], i["L1_attn_wk"], i["L1_attn_wv"]
    arrays = {
        "x": i["L0_attn_x"].reshape(TILES, P, D).transpose(1, 0, 2),
        "cT": _np.stack([i["L0_c"].T, i["L1_c"].T], axis=1),
        "wmod": _np.stack([i["L0_wmod"], i["L1_wmod"]], axis=1),
        "wg": i["L0_attn_Wg"].reshape(D, 1),
        "bg": i["L0_attn_bg"].reshape(1, 1),
        "woutT": i["L0_attn_Wout"].T,
        "bias_rows": _np.stack([i["L0_attn_bout"], i["L0_ffn_b2"], i["L1_ffn_b2"]])[None],
        "mb": i["L0_ffn_mb"].reshape(1, F),
        "m1T": i["L0_ffn_m1"].T,
        "m2": i["L0_ffn_m2"].reshape(DH, F),
        "w1": i["L0_ffn_w1"].reshape(D, F),
        "w2": i["L0_ffn_w2"].transpose(1, 0, 2).reshape(FC, P, D).transpose(1, 0, 2),
        "w_attn": _np.stack([wq.T, swapped(wq).T, wk.T, swapped(wk).T, wv.T]),
        "woT": i["L1_attn_wo"].T.reshape(PAIRS, P, D).transpose(1, 0, 2),
        "u1T": i["L1_ffn_U1"].T,
        "v1": i["L1_ffn_V1"],
        "u2T": i["L1_ffn_U2"].T,
        "v2": i["L1_ffn_V2"],
        "b1": i["L1_ffn_b1"].reshape(FC, P).T,
        **constants(),
    }
    arrays = {f"in_{k}_dram": _np.ascontiguousarray(v) for k, v in arrays.items()}
    nc = _bacc.Bacc("TRN2", target_bir_lowering=False, num_devices=1)
    args = {k[3:-5]: nc.dram_tensor(k, v.shape, _mybir.dt.from_np(v.dtype), kind="ExternalInput").ap()
            for k, v in arrays.items()}
    out = nc.dram_tensor("out_0_dram", (P, TILES, D), F32, kind="ExternalOutput").ap()
    program(nc, args, out)
    r = _run(nc, [arrays], core_ids=[0])
    got = r.results[0]["out_0_dram"]
    return _np.ascontiguousarray(_np.asarray(got).transpose(1, 0, 2).reshape(B, T, D))
```

```python
from contextlib import ExitStack

import numpy as np
import concourse.bass as bass
from concourse import mybir

ALU = mybir.AluOpType
ACT = mybir.ActivationFunctionType
AX_X = mybir.AxisListType.X
F32 = mybir.dt.float32
F32R = mybir.dt.float32r
BF16 = mybir.dt.bfloat16
F16 = mybir.dt.float16

P = 128
B, T, D = 16, 256, 128
NT = T // P
TILES = B * NT
F = 512
FC = F // P
GROUPS, PICK = 8, 64
H, DH = 16, 64
HALF = DH // 2
PAIRS = H // 2
EPS = 1e-5
ROOT_STEPS = 12
P_SCALE = 4096.0
ROWS = F + 3 * D
ROWS_SPLIT = 8
SWAP = [(i + 16) % 32 for i in range(32)]
WIDE = 4


class Signal:

    def __init__(self, ctx, nc, name, per_batch):
        self.sem = ctx.enter_context(nc.semaphore(name))
        self.per = per_batch

    def nth(self, t, n):
        return t * self.per + (self.per + n)

    def before(self, t, n):
        return t * self.per + n


def program(nc, a, out):
    ctx = ExitStack()
    with ctx:
        def sb(name, shape, dt=F32):
            return ctx.enter_context(nc.sbuf_tensor(name, shape, dt))

        def sem(name):
            return ctx.enter_context(nc.semaphore(name))

        signals = []

        def sig(name, per):
            signals.append(Signal(ctx, nc, name, per))
            return signals[-1]

        bank = [ctx.enter_context(nc.psum_tensor(f"bank{i}", [P, 512], F32)) for i in range(8)]

        x = sb("x", [P, TILES, D])
        ident = sb("ident", [P, P])
        ident_bf = sb("ident_bf", [P, P], BF16)
        causal = sb("causal", [P, P])
        causal_bf = sb("causal_bf", [P, P], BF16)
        first = sb("first", [P, P])
        first_bf = sb("first_bf", [P, P], BF16)
        rope_tab = sb("rope_tab", [P, 4, T])
        ones3 = sb("ones3", [3, P], BF16)
        cT = sb("cT", [P, 2, B])
        silu = sb("silu", [P, 2, B])
        silu_e = sb("silu_e", [P, 2, B])
        wmod = sb("wmod", [P, 2, 6 * D])
        modT = sb("modT", [P, 2, 4, B])
        gate_row = sb("gate_row", [B, 2, 2, D])
        gate = sb("gate", [P, 2, 2, B, D])
        gates0 = gate[:, 0, :, :, :].rearrange("p k r d -> p (k r d)")
        wg = sb("wg", [P, 1])
        bg = sb("bg", [P, 1])
        woutT = sb("woutT", [P, D])
        rows = sb("rows", [1, ROWS])
        rows_part = sb("rows_part", [1, 3, ROWS], BF16)
        rows3 = sb("rows3", [3, ROWS], BF16)
        m1T = sb("m1T", [DH, D])
        m2 = sb("m2", [DH, F])
        w_in = sb("w_in", [P, 2 * F])
        w_in_hi = sb("w_in_hi", [P, 2 * F], F32R)
        w_in_lo = sb("w_in_lo", [P, 2 * F], F32R)
        w2 = sb("w2", [P, FC, D])
        stage = sb("stage", [P, 2, H * DH])
        w_hi = sb("w_hi", [P, 3, H * DH], F32R)
        w_lo = sb("w_lo", [P, 3, H * DH], F32R)
        woT = sb("woT", [P, PAIRS, D])
        u1T = sb("u1T", [32, D])
        v1 = sb("v1", [32, F])
        u2T = sb("u2T", [32, F])
        v2 = sb("v2", [32, D])
        b1 = sb("b1", [P, FC])
        uv1 = sb("uv1", [P, F])
        uv2 = sb("uv2", [P, FC, D])

        stats = sb("stats", [P, TILES, 6])
        mean = sb("mean", [P, TILES])
        apart = sb("apart", [P, TILES])
        var = sb("var", [P, TILES])
        root = sb("root", [P, TILES])
        rstd = sb("rstd", [P, TILES])
        newton = sb("newton", [P, TILES])

        xn = sb("xn", [P, WIDE, NT, D])
        hT = sb("hT", [P, WIDE, T])
        hid = sb("hid", [P, WIDE, FC, T])
        hid_flat = hid[:, :, :, :].rearrange("p w c t -> p (w c t)")
        g, keep, gh, scanned = (hid[:, :, i, :] for i in range(4))
        step = sb("step", [P, WIDE, NT, D])

        h_hi = sb("h_hi", [P, 2, T], F32R)
        h_lo = sb("h_lo", [P, 2, T], F32R)
        top = sb("top", [P, NT, GROUPS])
        hits = sb("hits", [P, NT, F], BF16)
        hitsT = sb("hitsT", [P, FC, T], BF16)
        picked = sb("picked", [P, FC, T], BF16)

        val1 = sb("val1", [P, 2, NT, H, DH + 1], BF16)
        val2 = sb("val2", [P, 2, NT, H, DH], BF16)
        val3 = sb("val3", [P, 2, NT, H, DH], BF16)
        val_rest = [w_in[:, :], stage[:, 0, :]]
        rope_a = sb("rope_a", [P, 2, 2 * T])
        rope_b = sb("rope_b", [P, 2, 2 * T])
        rope_s = stage[:, 1, :].rearrange("p (b n) -> p b n", b=2)
        gate_hi, gate_lo, gate_a, gate_b = (
            r[0:B, i, :].rearrange("b (l k d) -> b l k d", l=2, k=2) for r in (rope_a, rope_b) for i in range(2))
        nmax = sb("nmax", [P, 4, NT])
        rsum = sb("rsum", [P, 2, 4])
        qk = gates0[:, 0:2048].rearrange("p (b a t) -> p b a t", b=4, a=2)
        oT = gates0[:, 2048:2560].rearrange("p (b t) -> p b t", b=2)
        probs = hid_flat[:, 0:1536].rearrange("p (b k) -> p b k", b=4)
        probsT_hi = hid_flat[:, 1536:2304].bitcast(F16).rearrange("p (b k) -> p b k", b=4)
        probsT_lo = hid_flat[:, 2304:3072].bitcast(F16).rearrange("p (b k) -> p b k", b=4)
        o = hid_flat[:, 3072:3584].rearrange("p (b j h d) -> p b j h d", b=2, j=NT, h=2)

        s_x = sem("x_loaded")
        s_mod = sem("modulation_weights_loaded")
        s_const = sem("constants_loaded")
        s_rows = sem("bias_rows_spread")
        s_w = [sem(f"attention_weights_loaded_{i}") for i in range(2)]
        s_out = sem("output_stored")
        pre_v = sem("prologue_vector")
        pre_s = sem("prologue_scalar")
        pre_t = sem("prologue_tensor")
        x_stats = sem("input_statistics")
        w_split = sem("attention_weight_split")
        w_in_split = sem("feed_forward_weight_split")
        st_v = sem("rstd_vector_step")
        st_s = sem("rstd_root")

        def phase(tag, **counts):
            return {k: sig(f"{tag}_{k}", v) for k, v in counts.items()}

        L1 = phase("scan", xn=WIDE, xT=WIDE, h=WIDE, z=WIDE, g=WIDE, keep=WIDE, gh=WIDE, scanned=WIDE,
                   y=WIDE, gated=WIDE, x=WIDE, stats=WIDE)
        L2 = phase("pick", xn=1, xT=1, h=1, hi=1, lo=1, logits=2, top=2, hits=2, hitsT_ps=1, hitsT=1,
                   first=1, picked=2, hidden=1, hid=2, y=1, gated=1, x=1, stats=1)
        L3 = phase("attn", xn=1, xT=1, h=1, hi=1, lo=1, v_ps=4, v1=4, rest=4, v2=4, v3=4, qk_ps=PAIRS,
                   turned=PAIRS, mul=PAIRS, mul2=PAIRS, rope=PAIRS, s=H, nmax=H, exp=H, pT=H, pT_hi=H, pT_lo=H,
                   pv=PAIRS, rsum=PAIRS, o=PAIRS, oT_ps=PAIRS, oT=PAIRS, y_add=PAIRS, gated=1, x=1, stats=1)
        L3["y"] = L3["y_add"]
        L4 = phase("gelu", xn=WIDE, xT=WIDE, h=WIDE, up=WIDE, act=WIDE * FC, y=WIDE, gated=WIDE, x=WIDE)

        MODS = [(cT, a["cT"]), (wmod, a["wmod"])]
        CONSTS = [
            (ident, a["ident"]), (wg, a["wg"]), (woutT, a["woutT"]), (rows, a["rows"]),
            (m1T, a["m1T"]), (m2, a["m2"]), (u1T, a["u1T"]), (v1, a["v1"]), (u2T, a["u2T"]), (v2, a["v2"]),
            (first, a["first"]), (causal, a["causal"]),
            (w2, a["w2"]), (b1, a["b1"]), (rope_tab, a["rope"]), (woT, a["woT"]),
        ]

        def full(tensor):
            return tensor[tuple(slice(None) for _ in tensor.shape)]

        block = ctx.enter_context(nc.Block())

        @block.sync
        def _(sp):
            for s in signals:
                sp.sem_inc(s.sem, s.per)
            for dst, src in MODS:
                sp.dma_start(full(dst), src).then_inc(s_mod, 16)
            for i in range(2):
                n = TILES // 2
                sp.dma_start(x[:, i * n:(i + 1) * n, :], a["x"][:, i * n:(i + 1) * n, :]).then_inc(s_x, 16)
            for dst, src in CONSTS[:len(CONSTS) // 2]:
                sp.dma_start(full(dst), src).then_inc(s_const, 16)
            sp.dma_start(w_in[:, F:2 * F], a["w1"]).then_inc(s_const, 16)
            sp.wait_ge(pre_v, ROWS_SPLIT)
            sp.dma_start(rows3[:, :], rows_part[0:1, :, :]).then_inc(s_rows, 16)
            sp.wait_ge(w_split, 2)
            sp.dma_start(stage[:, 0, :], a["w_attn"][2]).then_inc(s_w[0], 16)
            with sp.Fori(0, B // WIDE) as t:
                sp.wait_ge(L4["x"].sem, L4["x"].nth(t, WIDE))
                sp.dma_start(out[:, bass.ds(t * (WIDE * NT), WIDE * NT), :],
                             x[:, bass.ds(t * (WIDE * NT), WIDE * NT), :]).then_inc(s_out, 16)
            sp.wait_ge(s_out, 16 * (B // WIDE))

        N_CONST = 16 * (len(CONSTS) + 2)

        def row_tiles(t):
            return x[:, bass.ds(t * NT, NT), :]

        def ahead(t, n):
            return not isinstance(t, int) or t + n < B

        def neighbours(t, p):
            return t + p // PAIRS, p % PAIRS

        @block.vector
        def _(dve):
            dve.memset(ones3[:, :], 1.0).then_inc(pre_v, 1)
            dve.memset(val1[:, :, :, :, DH:DH + 1].rearrange("p b j h o -> p (b j h) o"), 1.0).then_inc(pre_v, 1)
            dve.wait_ge(pre_s, 1)
            dve.tensor_tensor(silu[:, :, :], cT[:, :, :], silu_e[:, :, :], ALU.mult).then_inc(pre_v, 1)
            dve.wait_ge(s_const, N_CONST)
            for i in range(3):
                dve.tensor_copy(rows_part[:, i, :], rows[:, :]).then_inc(pre_v, 1)
                if i < 2:
                    dve.wait_ge(pre_v, 4 + 2 * i)
                    dve.tensor_tensor(rows[:, :], rows[:, :], rows_part[:, i, :], ALU.subtract).then_inc(pre_v, 1)
                    dve.wait_ge(pre_v, 5 + 2 * i)
            dve.wait_ge(pre_t, 1)
            for l in range(2):
                for k in range(4):
                    dve.tensor_scalar(modT[:, l, k, :], bank[0][:, (l * 4 + k) * B:(l * 4 + k + 1) * B],
                                      float(k % 2), None, ALU.add).then_inc(pre_v, 1)
            raw = bank[1][0:B, :].rearrange("b (l k d) -> b l k d", l=2, k=2)
            dve.tensor_copy(gate_row[:, :, :, :], raw).then_inc(pre_v, 1)
            dve.wait_ge(pre_v, 17)
            dve.tensor_scalar(gate_hi, gate_row[:, :, :, :], 0.25, None, ALU.max).then_inc(pre_v, 1)
            dve.tensor_scalar(gate_lo, gate_row[:, :, :, :], -0.25, None, ALU.min).then_inc(pre_v, 1)
            dve.wait_ge(pre_v, 19)

            def flat(t):
                return t.rearrange("b l k d -> b (l k d)")

            dve.scalar_tensor_tensor(out=flat(gate_a), in0=flat(gate_row[:, :, :, :]), scalar=0.0,
                                     in1=flat(gate_hi), op0=ALU.is_ge, op1=ALU.mult).then_inc(pre_v, 1)
            dve.scalar_tensor_tensor(out=flat(gate_b), in0=flat(gate_row[:, :, :, :]), scalar=0.0,
                                     in1=flat(gate_lo), op0=ALU.is_lt, op1=ALU.mult).then_inc(pre_v, 1)
            dve.wait_ge(pre_v, 21)
            dve.tensor_tensor(flat(gate_row[:, :, :, :]), flat(gate_a), flat(gate_b), ALU.add).then_inc(pre_v, 1)
            dve.wait_ge(s_x, 32)
            for i in range(TILES):
                dve.bn_stats(stats[:, i, :], x[:, i, :]).then_inc(x_stats, 1)
            dve.wait_ge(x_stats, TILES)

            def finish_rstd(n):
                done = [ROOT_STEPS * n]

                def then(ins, wait=True):
                    ins.then_inc(st_v, 1)
                    done[0] += 1
                    if wait:
                        dve.wait_ge(st_v, done[0])

                then(dve.tensor_tensor(apart[:, :], stats[:, :, 1], stats[:, :, 4], ALU.subtract), False)
                then(dve.tensor_tensor(mean[:, :], stats[:, :, 1], stats[:, :, 4], ALU.add), False)
                then(dve.tensor_tensor(var[:, :], stats[:, :, 2], stats[:, :, 5], ALU.add))
                then(dve.scalar_tensor_tensor(out=apart[:, :], in0=apart[:, :], scalar=0.25, in1=apart[:, :],
                                              op0=ALU.mult, op1=ALU.mult), False)
                then(dve.tensor_scalar(var[:, :], var[:, :], 1.0 / D, EPS, ALU.mult, ALU.add))
                then(dve.tensor_scalar(mean[:, :], mean[:, :], 0.5, None, ALU.mult), False)
                then(dve.tensor_tensor(var[:, :], var[:, :], apart[:, :], ALU.add))
                dve.wait_ge(st_s, n + 1)
                then(dve.reciprocal(rstd[:, :], root[:, :]))
                then(dve.tensor_tensor(newton[:, :], var[:, :], rstd[:, :], ALU.mult))
                then(dve.tensor_tensor(newton[:, :], newton[:, :], rstd[:, :], ALU.mult))
                then(dve.tensor_scalar(newton[:, :], newton[:, :], -0.5, 1.5, ALU.mult, ALU.add))
                then(dve.tensor_tensor(rstd[:, :], rstd[:, :], newton[:, :], ALU.mult))
                assert done[0] == ROOT_STEPS * (n + 1)

            def normalise(S, t, w, row, nth):
                dve.wait_ge(S["xT"].sem, S["xT"].before(t, nth))
                for j in range(NT):
                    i = row * NT + j
                    last = dve.tensor_scalar(
                        xn[:, w, j, :], x[:, bass.ds(i, 1), :].rearrange("p o d -> p (o d)"),
                        mean[:, bass.ds(i, 1)], rstd[:, bass.ds(i, 1)], ALU.subtract, ALU.mult)
                last.then_inc(S["xn"].sem, 1)

            def modulate(S, t, w, row, nth, psum, l, k):
                dve.wait_ge(S["xT"].sem, S["xT"].nth(t, nth))
                dve.tensor_scalar(hT[:, w, :], psum[:, 0:T], modT[:, l, 2 * k + 1, bass.ds(row, 1)],
                                  modT[:, l, 2 * k, bass.ds(row, 1)], ALU.mult, ALU.add).then_inc(S["h"].sem, 1)

            def add_gated(S, t, w, row, nth, psum, l, k, with_stats=True, y=None):
                dve.wait_ge(S["y"].sem, S["y"].nth(t, y or nth))
                gate_bc = gate[:, l, k, bass.ds(row, 1), :].to_broadcast([P, NT, D])
                dve.tensor_tensor(step[:, w, :, :], psum.rearrange("p (j d) -> p j d", j=NT), gate_bc, ALU.mult)\
                   .then_inc(S["gated"].sem, 1)
                dve.wait_ge(S["gated"].sem, S["gated"].nth(t, nth))
                dve.tensor_tensor(row_tiles(row), row_tiles(row), step[:, w, :, :], ALU.add).then_inc(S["x"].sem, 1)
                if not with_stats:
                    return
                dve.wait_ge(S["x"].sem, S["x"].nth(t, nth))
                for j in range(NT):
                    i = row * NT + j
                    last = dve.bn_stats(stats[:, bass.ds(i, 1), :].rearrange("p o s -> p (o s)"),
                                        x[:, bass.ds(i, 1), :].rearrange("p o d -> p (o d)"))
                last.then_inc(S["stats"].sem, 1)

            def scan_ahead(t):
                for w in range(WIDE):
                    normalise(L1, t, w, t * WIDE + w, w + 1)
                for w in range(WIDE):
                    dve.wait_ge(L1["z"].sem, L1["z"].before(t, w + 1))
                    modulate(L1, t, w, t * WIDE + w, w + 1, bank[2 * w + 1], 0, 0)

            def scan_group(t, more):
                for w in range(WIDE):
                    dve.wait_ge(L1["g"].sem, L1["g"].nth(t, w + 1))
                    dve.wait_ge(L1["scanned"].sem, L1["scanned"].before(t, w + 1))
                    dve.tensor_scalar(keep[:, w, :], g[:, w, :], -1.0, 1.0, ALU.mult, ALU.add)\
                       .then_inc(L1["keep"].sem, 1)
                    dve.tensor_tensor(gh[:, w, :], g[:, w, :], hT[:, w, :], ALU.mult).then_inc(L1["gh"].sem, 1)
                    dve.wait_ge(L1["keep"].sem, L1["keep"].nth(t, w + 1))
                    dve.wait_ge(L1["gh"].sem, L1["gh"].nth(t, w + 1))
                    dve.wait_ge(L1["y"].sem, L1["y"].before(t, w + 1))
                    dve.tensor_tensor_scan(scanned[:, w, :], keep[:, w, :], gh[:, w, :], 0.0,
                                           ALU.mult, ALU.add).then_inc(L1["scanned"].sem, 1)
                if more:
                    scan_ahead(t + 1)
                for w in range(WIDE):
                    add_gated(L1, t, w, t * WIDE + w, w + 1, bank[2 * w][:, 0:T], 0, 0)

            finish_rstd(0)
            dve.wait_ge(pre_v, 16)
            scan_ahead(0)
            with dve.Fori(0, B // WIDE - 1) as t:
                scan_group(t, True)
            scan_group(B // WIDE - 1, False)
            dve.wait_ge(L1["stats"].sem, L1["stats"].nth(B // WIDE - 1, WIDE))

            def find_hits(t, j):
                groups = bank[1 + j][:, :].rearrange("p (g k) -> p g k", g=GROUPS)
                dve.wait_ge(L2["logits"].sem, L2["logits"].nth(t, j + 1))
                dve.wait_ge(L2["hitsT_ps"].sem, L2["hitsT_ps"].before(t, 1))
                dve.tensor_reduce(top[:, j, :], groups, AX_X, ALU.max).then_inc(L2["top"].sem, 1)
                dve.wait_ge(L2["top"].sem, L2["top"].nth(t, j + 1))
                dve.tensor_tensor(hits[:, j, :].rearrange("p (g k) -> p g k", g=GROUPS), groups,
                                  top[:, j, :].unsqueeze(2).to_broadcast([P, GROUPS, PICK]),
                                  ALU.is_ge).then_inc(L2["hits"].sem, 1)

            def pick_row(t, par):
                if ahead(t, 2):
                    normalise(L2, t + 2, par, t + 2, 1)
                if ahead(t, 1):
                    for j in range(NT):
                        find_hits(t + 1, j)
                for c2 in range(2):
                    dve.wait_ge(L2["hidden"].sem, L2["hidden"].nth(t, 1))
                    dve.wait_ge(L2["picked"].sem, L2["picked"].nth(t, c2 + 1))
                    dve.wait_ge(L2["y"].sem, L2["y"].before(t, 1))
                    dve.scalar_tensor_tensor(
                        out=hid[:, 0, 2 * c2:2 * c2 + 2, :].rearrange("p c t -> p (c t)"),
                        in0=bank[6 + c2][:, :], scalar=0.0,
                        in1=picked[:, 2 * c2:2 * c2 + 2, :].rearrange("p c t -> p (c t)"),
                        op0=ALU.max, op1=ALU.mult).then_inc(L2["hid"].sem, 1)
                add_gated(L2, t, par, t, 1, bank[3][:, 0:T], 0, 1)

            finish_rstd(1)
            normalise(L2, 0, 0, 0, 1)
            normalise(L2, 1, 1, 1, 1)
            for j in range(NT):
                find_hits(0, j)
            with dve.Fori(0, B // 2 - 1) as i:
                pick_row(2 * i, 0)
                pick_row(2 * i + 1, 1)
            pick_row(B - 2, 0)
            pick_row(B - 1, 1)
            dve.wait_ge(L2["stats"].sem, L2["stats"].nth(B - 1, 1))

            def v_rest(t, u, par):
                heads = slice((u % 2) * 8, (u % 2) * 8 + 8)
                dve.wait_ge(L3["v1"].sem, L3["v1"].nth(t, u + 1))
                dve.wait_ge(L3["v3"].sem, L3["v3"].before(t, u + 1))
                dve.tensor_tensor(val_rest[u // 2][:, (u % 2) * 512:(u % 2 + 1) * 512]
                                  .rearrange("p (h d) -> p h d", h=8),
                                  bank[1 - u % 2][:, :].rearrange("p (h d) -> p h d", h=8),
                                  val1[:, par, u // 2, heads, 0:DH], ALU.subtract).then_inc(L3["rest"].sem, 1)

            def rotate(t, p):
                dve.wait_ge(L3["qk_ps"].sem, L3["qk_ps"].nth(t, p + 1))
                was = neighbours(t - 1, p + PAIRS - 2)
                dve.wait_ge(L3["rope"].sem, L3["rope"].nth(was[0], was[1] + 1))
                ps = bank[p % 2][:, :]
                dve.tensor_tensor(rope_a[:, p % 2, :], ps, rope_tab[:, 0:2, :].rearrange("p a t -> p (a t)"),
                                  ALU.mult).then_inc(L3["mul"].sem, 1)
                dve.stream_shuffle(rope_s[:, p % 2, :], ps, SWAP).then_inc(L3["turned"].sem, 1)

            def row_max(t, h):
                s = bank[2 + h % 2]
                dve.wait_ge(L3["s"].sem, L3["s"].nth(t, h + 1))
                was = neighbours2(t - 1, h + H - 4)
                dve.wait_ge(L3["exp"].sem, L3["exp"].nth(was[0], was[1] + 1))
                dve.tensor_reduce(nmax[:, h % 4, 0:1], s[:, 0:P], AX_X, ALU.max, negate=True)
                dve.tensor_reduce(nmax[:, h % 4, 1:2], s[:, P:3 * P], AX_X, ALU.max, negate=True)\
                   .then_inc(L3["nmax"].sem, 1)

            def low_part(t, h):
                dve.wait_ge(L3["pT_hi"].sem, L3["pT_hi"].nth(t, h + 1))
                dve.scalar_tensor_tensor(out=probsT_lo[:, h % 4, :], in0=bank[4 + h % 2][:, 0:3 * P],
                                         scalar=P_SCALE, in1=probsT_hi[:, h % 4, :],
                                         op0=ALU.mult, op1=ALU.subtract).then_inc(L3["pT_lo"].sem, 1)

            def divide(t, p):
                ov = bank[6][:, 0:4 * (DH + 1)].rearrange("p (q d) -> p q d", q=4)
                dve.wait_ge(L3["pv"].sem, L3["pv"].nth(t, p + 1))
                dve.reciprocal(rsum[:, p % 2, :], ov[:, :, DH]).then_inc(L3["rsum"].sem, 1)
                dve.wait_ge(L3["rsum"].sem, L3["rsum"].nth(t, p + 1))
                dve.tensor_tensor(o[:, p % 2, :, :, :].rearrange("p j h d -> p (j h) d"), ov[:, :, 0:DH],
                                  rsum[:, p % 2, :].unsqueeze(2).to_broadcast([P, 4, DH]), ALU.mult)\
                   .then_inc(L3["o"].sem, 1)

            def turn_tiles(t):
                dve.wait_ge(L3["lo"].sem, L3["lo"].before(t, 1))
                dve.wait_ge(L3["xT"].sem, L3["xT"].nth(t, 1))
                for j in range(NT):
                    last = dve.tensor_scalar(hT[:, 0, j * P:(j + 1) * P], bank[4 + j][:, 3 * P:4 * P],
                                             modT[:, 1, 1, bass.ds(t, 1)], modT[:, 1, 0, bass.ds(t, 1)],
                                             ALU.mult, ALU.add)
                last.then_inc(L3["h"].sem, 1)

            def attend_row(t, par, more, start=False):
                for p in range(PAIRS):
                    if not start:
                        low_part(t, 2 * p)
                        low_part(t, 2 * p + 1)
                    if more and p == 0:
                        normalise(L3, t + 1, 0, t + 1, 1)
                    if more and p == 1:
                        turn_tiles(t + 1)
                    if not start and p + 1 < PAIRS:
                        row_max(t, 2 * p + 2)
                        row_max(t, 2 * p + 3)
                    if more and p == PAIRS - 1:
                        row_max(t + 1, 0)
                        row_max(t + 1, 1)
                    if not start and p + 3 < PAIRS:
                        rotate(t, p + 3)
                    if more and p + 3 >= PAIRS:
                        rotate(t + 1, p + 3 - PAIRS)
                    if more and 3 <= p < 7:
                        v_rest(t + 1, p - 3, 1 - par)
                    if not start:
                        divide(t, p)
                if start:
                    return
                add_gated(L3, t, 0, t, 1, bank[7][:, 0:T], 1, 0, y=PAIRS)

            def neighbours2(t, h):
                return t + h // H, h % H

            finish_rstd(2)
            attend_row(-1, 1, True, start=True)
            with dve.Fori(0, B // 2 - 1) as i:
                attend_row(2 * i, 0, True)
                attend_row(2 * i + 1, 1, True)
            attend_row(B - 2, 0, True)
            attend_row(B - 1, 1, False)
            dve.wait_ge(L3["stats"].sem, L3["stats"].nth(B - 1, 1))

            def gelu_ahead(t):
                for w in range(WIDE):
                    normalise(L4, t, w, t * WIDE + w, w + 1)

            def gelu_group(t, more):
                for w in range(WIDE):
                    dve.wait_ge(L4["up"].sem, L4["up"].before(t, w + 1))
                    modulate(L4, t, w, t * WIDE + w, w + 1, bank[4 + w], 1, 1)
                if more:
                    gelu_ahead(t + 1)
                for w in range(WIDE):
                    add_gated(L4, t, w, t * WIDE + w, w + 1, bank[4 + w][:, 0:T], 1, 1, with_stats=False)

            finish_rstd(3)
            gelu_ahead(0)
            with dve.Fori(0, B // WIDE - 1) as t:
                gelu_group(t, True)
            gelu_group(B // WIDE - 1, False)

        @block.scalar
        def _(act):
            for dst, src in CONSTS[len(CONSTS) // 2:]:
                act.dma_start(full(dst), src).then_inc(s_const, 16)
            act.dma_start(bg[:, :], a["bg"].to_broadcast([P, 1])).then_inc(s_const, 16)
            for i in range(2):
                act.dma_start(stage[:, i, :], a["w_attn"][i]).then_inc(s_w[i], 16)
            act.wait_ge(s_mod, 32)
            act.activation(silu_e[:, :, :], cT[:, :, :], ACT.Sigmoid).then_inc(pre_s, 1)
            for n in range(B):
                l, k, q = n // 8, n // 4 % 2, n % 4
                act.wait_ge(pre_t, 3 + n)
                act.activation(gate[:, l, k, 4 * q:4 * q + 4, :],
                               bank[n % 8][:, :].rearrange("p (r d) -> p r d", r=4), ACT.Copy).then_inc(pre_s, 1)
                if n == 3:
                    act.activation(w_in[:, 0:F], bank[5][:, :], ACT.Copy).then_inc(pre_s, 1)
                    act.activation(uv1[:, :], bank[6][:, :], ACT.Copy).then_inc(pre_s, 1)
                    act.activation(uv2[:, :, :], bank[7][:, :].rearrange("p (c d) -> p c d", c=FC), ACT.Copy)\
                       .then_inc(pre_s, 1)

            def roots(n):
                act.wait_ge(st_v, ROOT_STEPS * n + 7)
                act.activation(root[:, :], var[:, :], ACT.Sqrt).then_inc(st_s, 1)

            roots(0)
            with act.Fori(0, B // WIDE) as t:
                for w in range(WIDE):
                    act.wait_ge(L1["z"].sem, L1["z"].nth(t, w + 1))
                    act.wait_ge(L1["gh"].sem, L1["gh"].before(t, w + 1))
                    act.activation(g[:, w, :], bank[2 * w + 1][:, 0:T], ACT.Sigmoid, bias=bg[:, 0:1])\
                       .then_inc(L1["g"].sem, 1)

            def modulate_split(t, par):
                act.wait_ge(L2["xT"].sem, L2["xT"].nth(t, 1))
                act.wait_ge(L2["lo"].sem, L2["lo"].before(t, 1))
                act.wait_ge(L2["hidden"].sem, L2["hidden"].before(t - 1, 1))
                shift, scale = modT[:, 0, 2, bass.ds(t, 1)], modT[:, 0, 3, bass.ds(t, 1)]
                act.activation(hT[:, 0, :], bank[0][:, 0:T], ACT.Identity, bias=shift, scale=scale)\
                   .then_inc(L2["h"].sem, 1)
                act.activation(h_hi[:, par, :], bank[0][:, 0:T], ACT.Identity, bias=shift, scale=scale)\
                   .then_inc(L2["hi"].sem, 1)

            def pick_row(t, par):
                act.wait_ge(L2["hitsT_ps"].sem, L2["hitsT_ps"].nth(t, 1))
                act.wait_ge(L2["first"].sem, L2["first"].before(t, 1))
                act.activation(hitsT[:, :, :].rearrange("p c t -> p (c t)"), bank[3][:, :].bitcast(BF16), ACT.Copy)\
                   .then_inc(L2["hitsT"].sem, 1)
                act.wait_ge(L2["first"].sem, L2["first"].nth(t, 1))
                for c2 in range(2):
                    act.wait_ge(L2["hid"].sem, L2["hid"].before(t, c2 + 1))
                    act.activation(picked[:, 2 * c2:2 * c2 + 2, :].rearrange("p c t -> p (c t)"),
                                   bank[4 + c2][:, :], ACT.Relu).then_inc(L2["picked"].sem, 1)
                if ahead(t, 2):
                    modulate_split(t + 2, par)

            roots(1)
            modulate_split(0, 0)
            modulate_split(1, 1)
            with act.Fori(0, B // 2 - 1) as i:
                pick_row(2 * i, 0)
                pick_row(2 * i + 1, 1)
            pick_row(B - 2, 0)
            pick_row(B - 1, 1)
            roots(2)

            def v_part(t, u, par):
                heads = slice((u % 2) * 8, (u % 2) * 8 + 8)
                act.wait_ge(L3["v_ps"].sem, L3["v_ps"].nth(t, u + 1))
                act.activation(val1[:, par, u // 2, heads, 0:DH],
                               bank[1 - u % 2][:, :].rearrange("p (h d) -> p h d", h=8), ACT.Copy)\
                   .then_inc(L3["v1"].sem, 1)

            def v_part2(t, u, par):
                heads = slice((u % 2) * 8, (u % 2) * 8 + 8)
                act.wait_ge(L3["rest"].sem, L3["rest"].nth(t, u + 1))
                act.activation(val2[:, par, u // 2, heads, :],
                               val_rest[u // 2][:, (u % 2) * 512:(u % 2 + 1) * 512]
                               .rearrange("p (h d) -> p h d", h=8), ACT.Copy).then_inc(L3["v2"].sem, 1)

            def high_part(t, h):
                act.wait_ge(L3["pT"].sem, L3["pT"].nth(t, h + 1))
                was = neighbours(t - 1, h // 2 + PAIRS - 2)
                act.wait_ge(L3["pv"].sem, L3["pv"].nth(was[0], was[1] + 1))
                act.activation(probsT_hi[:, h % 4, :], bank[4 + h % 2][:, 0:3 * P], ACT.Copy,
                               scale=P_SCALE).then_inc(L3["pT_hi"].sem, 1)

            def exps(t, h):
                s = bank[2 + h % 2]
                act.wait_ge(L3["nmax"].sem, L3["nmax"].nth(t, h + 1))
                was = t - 1 + (h + H - 4) // H, (h + H - 4) % H
                act.wait_ge(L3["pT"].sem, L3["pT"].nth(was[0], was[1] + 1))
                act.activation(probs[:, h % 4, 0:P], s[:, 0:P], ACT.Exp, bias=nmax[:, h % 4, 0:1])
                act.activation(probs[:, h % 4, P:3 * P], s[:, P:3 * P], ACT.Exp, bias=nmax[:, h % 4, 1:2])\
                   .then_inc(L3["exp"].sem, 1)

            def heads_out(t, p):
                act.wait_ge(L3["oT_ps"].sem, L3["oT_ps"].nth(t, p + 1))
                was = neighbours(t - 1, p + PAIRS - 2)
                act.wait_ge(L3["y_add"].sem, L3["y_add"].nth(was[0], was[1] + 1))
                act.activation(oT[:, p % 2, :], bank[6][:, 0:T], ACT.Copy).then_inc(L3["oT"].sem, 1)

            def round_h(t, par):
                act.wait_ge(L3["h"].sem, L3["h"].nth(t, 1))
                act.wait_ge(L3["qk_ps"].sem, L3["qk_ps"].before(t, 1))
                act.activation(h_hi[:, par, :], hT[:, 0, :], ACT.Copy).then_inc(L3["hi"].sem, 1)

            def attend_row(t, par, more, start=False):
                for p in range(PAIRS):
                    if not start:
                        high_part(t, 2 * p)
                        high_part(t, 2 * p + 1)
                    if more and p == 2:
                        round_h(t + 1, 1 - par)
                    if more and 4 <= p < 8:
                        v_part2(t + 1, p - 4, 1 - par)
                    if not start and p >= 1:
                        heads_out(t, p - 1)
                    if not start and p + 1 < PAIRS:
                        exps(t, 2 * p + 2)
                        exps(t, 2 * p + 3)
                    if more and p == PAIRS - 1:
                        exps(t + 1, 0)
                        exps(t + 1, 1)
                    if more and 3 <= p < 7:
                        v_part(t + 1, p - 3, 1 - par)
                if not start:
                    heads_out(t, PAIRS - 1)

            attend_row(-1, 1, True, start=True)
            with act.Fori(0, B // 2 - 1) as i:
                attend_row(2 * i, 0, True)
                attend_row(2 * i + 1, 1, True)
            attend_row(B - 2, 0, True)
            attend_row(B - 1, 1, False)
            roots(3)
            with act.Fori(0, B // WIDE) as t:
                for w in range(WIDE):
                    act.wait_ge(L4["y"].sem, L4["y"].before(t, w + 1))
                    act.wait_ge(L4["up"].sem, L4["up"].nth(t, w + 1))
                    for c in range(FC):
                        act.activation(hid[:, w, c, :], bank[2 * (w % 2) + c // 2][:, (c % 2) * T:(c % 2 + 1) * T],
                                       ACT.Gelu_apprx_tanh, bias=b1[:, c:c + 1]).then_inc(L4["act"].sem, 1)

        @block.gpsimd
        def _(pool):
            pool.wait_ge(s_const, N_CONST)
            pool.tensor_copy(ident_bf[:, :], ident[:, :]).then_inc(w_in_split, 1)
            pool.tensor_copy(first_bf[:, :], first[:, :]).then_inc(w_in_split, 1)
            pool.tensor_copy(causal_bf[:, :], causal[:, :]).then_inc(w_in_split, 1)
            pool.wait_ge(pre_s, 6)
            pool.tensor_copy(w_in_hi[:, :], w_in[:, :]).then_inc(w_in_split, 1)
            pool.wait_ge(w_in_split, 4)
            pool.tensor_tensor(w_in_lo[:, :], w_in[:, :], w_in_hi[:, :].bitcast(F32), ALU.subtract)\
                .then_inc(w_in_split, 1)
            for i in range(3):
                pool.wait_ge(s_w[i % 2], 16 * (i // 2 + 1))
                pool.tensor_copy(w_hi[:, i, :], stage[:, i % 2, :]).then_inc(w_split, 1)
                pool.wait_ge(w_split, 2 * i + 1)
                pool.tensor_tensor(w_lo[:, i, :], stage[:, i % 2, :], w_hi[:, i, :].bitcast(F32),
                                   ALU.subtract).then_inc(w_split, 1)

            with pool.Fori(0, B // 2) as i:
                for par in range(2):
                    t = 2 * i + par
                    pool.wait_ge(L2["hi"].sem, L2["hi"].nth(t, 1))
                    pool.wait_ge(L2["hidden"].sem, L2["hidden"].before(t - 1, 1))
                    pool.tensor_tensor(h_lo[:, par, :], hT[:, 0, :], h_hi[:, par, :].bitcast(F32), ALU.subtract)\
                        .then_inc(L2["lo"].sem, 1)

            def v_part3(t, u, par):
                part = (slice(None), par, u // 2, slice((u % 2) * 8, (u % 2) * 8 + 8), slice(None))
                pool.wait_ge(L3["v2"].sem, L3["v2"].nth(t, u + 1))
                pool.tensor_tensor(val3[part], val_rest[u // 2][:, (u % 2) * 512:(u % 2 + 1) * 512]
                                   .rearrange("p (h d) -> p h d", h=8), val2[part], ALU.subtract)\
                    .then_inc(L3["v3"].sem, 1)

            def rope(t, p):
                pool.wait_ge(L3["turned"].sem, L3["turned"].nth(t, p + 1))
                pool.tensor_tensor(rope_b[:, p % 2, :], rope_s[:, p % 2, :],
                                   rope_tab[:, 2:4, :].rearrange("p a t -> p (a t)"), ALU.mult)\
                    .then_inc(L3["mul2"].sem, 1)
                pool.wait_ge(L3["mul2"].sem, L3["mul2"].nth(t, p + 1))
                was = neighbours(t - 1, p + PAIRS - 4)
                pool.wait_ge(L3["s"].sem, L3["s"].nth(was[0], 2 * was[1] + 2))
                pool.tensor_tensor(qk[:, p % 4, :, :].rearrange("p a t -> p (a t)"), rope_a[:, p % 2, :],
                                   rope_b[:, p % 2, :], ALU.add).then_inc(L3["rope"].sem, 1)

            def split_h(t, par):
                pool.wait_ge(L3["h"].sem, L3["h"].nth(t, 1))
                pool.wait_ge(L3["hi"].sem, L3["hi"].nth(t, 1))
                pool.tensor_tensor(h_lo[:, par, :], hT[:, 0, :], h_hi[:, par, :].bitcast(F32), ALU.subtract)\
                    .then_inc(L3["lo"].sem, 1)

            def attend_row(t, par, more, start=False):
                for p in range(PAIRS):
                    if more and p == 2:
                        split_h(t + 1, 1 - par)
                    if not start and p + 3 < PAIRS:
                        rope(t, p + 3)
                    if more and p + 3 >= PAIRS:
                        rope(t + 1, p + 3 - PAIRS)
                    if more and 4 <= p < 8:
                        v_part3(t + 1, p - 4, 1 - par)

            attend_row(-1, 1, True, start=True)
            with pool.Fori(0, B // 2 - 1) as i:
                attend_row(2 * i, 0, True)
                attend_row(2 * i + 1, 1, True)
            attend_row(B - 2, 0, True)
            attend_row(B - 1, 1, False)

        @block.tensor
        def _(pe):
            pe.wait_ge(pre_v, 3)
            pe.wait_ge(s_mod, 32)
            for l in range(2):
                for k, part in enumerate((0, 1, 3, 4)):
                    pe.matmul(bank[0][:, (l * 4 + k) * B:(l * 4 + k + 1) * B],
                              wmod[:, l, part * D:(part + 1) * D], silu[:, l, :], start=True, stop=True)
                for k, part in enumerate((2, 5)):
                    last = pe.matmul(bank[1][0:B, (l * 2 + k) * D:(l * 2 + k + 1) * D], silu[:, l, :],
                                     wmod[:, l, part * D:(part + 1) * D], start=True, stop=True)
            last.then_inc(pre_t, 1)
            pe.wait_ge(s_const, N_CONST)
            pe.matmul(bank[5][:, :], m1T[:, :], m2[:, :], start=True, stop=True)
            pe.matmul(bank[6][:, :], u1T[:, :], v1[:, :], start=True, stop=True)
            for c in range(FC):
                last = pe.matmul(bank[7][:, c * D:(c + 1) * D], u2T[:, c * P:(c + 1) * P], v2[:, :],
                                 start=True, stop=True)
            last.then_inc(pre_t, 1)
            pe.wait_ge(pre_v, 22)
            for n in range(B):
                l, k, q = n // 8, n // 4 % 2, n % 4
                if n >= 8:
                    pe.wait_ge(pre_s, 1 + 3 + n - 7)
                elif n >= 5:
                    pe.wait_ge(pre_s, 1 + 4 + n - 4)
                for r in range(4):
                    last = pe.matmul(bank[n % 8][:, r * D:(r + 1) * D],
                                     ident[0:B, 4 * q + r:4 * q + r + 1].to_broadcast([B, P]),
                                     gate_row[:, l, k, :], start=True, stop=True)
                last.then_inc(pre_t, 1)

            def to_d_major(S, t, w, nth, psum):
                pe.wait_ge(S["xn"].sem, S["xn"].nth(t, nth))
                for j in range(NT):
                    last = pe.transpose(psum[:, j * P:(j + 1) * P], xn[:, w, j, :], ident[:, :])
                last.then_inc(S["xT"].sem, 1)

            def bias(psum, k):
                return pe.matmul(psum, ones3[:, :], rows3[:, F + k * D:F + (k + 1) * D], start=False, stop=True)

            def scan_ahead(t):
                for w in range(WIDE):
                    pe.wait_ge(L1["g"].sem, L1["g"].before(t, w + 1))
                    to_d_major(L1, t, w, w + 1, bank[2 * w + 1])

            def scan_group(t, more):
                for w in range(WIDE):
                    pe.wait_ge(L1["h"].sem, L1["h"].nth(t, w + 1))
                    pe.matmul(bank[2 * w + 1][:, 0:T], wg[:, 0:1].to_broadcast([P, P]), hT[:, w, :],
                              start=True, stop=True).then_inc(L1["z"].sem, 1)
                for w in range(WIDE):
                    pe.wait_ge(L1["gated"].sem, L1["gated"].before(t, w + 1))
                    pe.wait_ge(L1["scanned"].sem, L1["scanned"].nth(t, w + 1))
                    for j in range(NT):
                        ps = bank[2 * w][:, j * P:(j + 1) * P]
                        pe.matmul(ps, scanned[:, w, j * P:(j + 1) * P], woutT[:, :], start=True, stop=False)
                        last = bias(ps, 0)
                    last.then_inc(L1["y"].sem, 1)
                if more:
                    scan_ahead(t + 1)

            pe.wait_ge(pre_s, 1 + 3 + B)
            scan_ahead(0)
            pe.wait_ge(s_rows, 16)
            with pe.Fori(0, B // WIDE - 1) as t:
                scan_group(t, True)
            scan_group(B // WIDE - 1, False)

            def find_logits(t, par):
                pe.wait_ge(L2["hi"].sem, L2["hi"].nth(t, 1))
                pe.wait_ge(L2["lo"].sem, L2["lo"].nth(t, 1))
                for j in range(NT):
                    tok = slice(j * P, (j + 1) * P)
                    ps = bank[1 + j][:, :]
                    pe.wait_ge(L2["hits"].sem, L2["hits"].before(t, j + 1))
                    pe.matmul(ps, h_hi[:, par, tok], w_in_hi[:, 0:F], start=True, stop=False)
                    pe.matmul(ps, h_hi[:, par, tok], w_in_lo[:, 0:F], start=False, stop=False)
                    pe.matmul(ps, h_lo[:, par, tok], w_in_hi[:, 0:F], start=False, stop=False)
                    pe.matmul(ps, ones3[:, :], rows3[:, 0:F], start=False, stop=True)\
                      .then_inc(L2["logits"].sem, 1)

            def find_hidden(t, par):
                pe.wait_ge(L2["hid"].sem, L2["hid"].before(t, 2))
                for c in range(FC):
                    f = slice(F + c * P, F + (c + 1) * P)
                    ps = bank[6 + c // 2][:, (c % 2) * T:(c % 2 + 1) * T]
                    pe.matmul(ps, w_in_hi[:, f], h_hi[:, par, :], start=True, stop=False)
                    pe.matmul(ps, w_in_hi[:, f], h_lo[:, par, :], start=False, stop=False)
                    last = pe.matmul(ps, w_in_lo[:, f], h_hi[:, par, :], start=False, stop=True)
                last.then_inc(L2["hidden"].sem, 1)

            def pick_row(t, par):
                hits_ps = bank[3][:, :].bitcast(BF16)
                pe.wait_ge(L2["gated"].sem, L2["gated"].before(t, 1))
                for j in range(NT):
                    pe.wait_ge(L2["hits"].sem, L2["hits"].nth(t, j + 1))
                    for c in range(FC):
                        last = pe.transpose(hits_ps[:, c * T + j * P:c * T + (j + 1) * P],
                                            hits[:, j, c * P:(c + 1) * P], ident_bf[:, :])
                last.then_inc(L2["hitsT_ps"].sem, 1)
                if ahead(t, 1):
                    find_logits(t + 1, 1 - par)
                pe.wait_ge(L2["hitsT"].sem, L2["hitsT"].nth(t, 1))
                pe.wait_ge(L2["picked"].sem, L2["picked"].before(t, 2))
                for c in range(FC):
                    last = pe.matmul(bank[4 + c // 2][:, (c % 2) * T:(c % 2 + 1) * T], first_bf[:, :],
                                     hitsT[:, c, :], start=True, stop=True)
                last.then_inc(L2["first"].sem, 1)
                if ahead(t, 2):
                    pe.wait_ge(L2["hi"].sem, L2["hi"].nth(t + 1, 1))
                    to_d_major(L2, t + 2, par, 1, bank[0])
                pe.wait_ge(L2["hid"].sem, L2["hid"].nth(t, 2))
                for j in range(NT):
                    ps = bank[3][:, j * P:(j + 1) * P]
                    for c in range(FC):
                        pe.matmul(ps, hid[:, 0, c, j * P:(j + 1) * P], w2[:, c, :], start=(c == 0), stop=False)
                    last = bias(ps, 1)
                last.then_inc(L2["y"].sem, 1)
                if ahead(t, 1):
                    find_hidden(t + 1, 1 - par)

            to_d_major(L2, 0, 0, 1, bank[0])
            pe.wait_ge(L2["hi"].sem, L2["hi"].nth(0, 1))
            to_d_major(L2, 1, 1, 1, bank[0])
            pe.wait_ge(w_in_split, 5)
            find_logits(0, 0)
            find_hidden(0, 0)
            with pe.Fori(0, B // 2 - 1) as i:
                pick_row(2 * i, 0)
                pick_row(2 * i + 1, 1)
            pick_row(B - 2, 0)
            pick_row(B - 1, 1)

            def project_v(t, u, par):
                tok = slice(u // 2 * P, (u // 2 + 1) * P)
                cols = slice((u % 2) * 512, (u % 2 + 1) * 512)
                if u == 0:
                    pe.wait_ge(L3["lo"].sem, L3["lo"].nth(t, 1))
                was = neighbours(t - 1, u + 5)
                pe.wait_ge(L3["turned"].sem, L3["turned"].nth(was[0], was[1] + 1))
                ps = bank[1 - u % 2][:, :]
                pe.matmul(ps, h_hi[:, par, tok], w_hi[:, 2, cols], start=True, stop=False)
                pe.matmul(ps, h_hi[:, par, tok], w_lo[:, 2, cols], start=False, stop=False)
                pe.matmul(ps, h_lo[:, par, tok], w_hi[:, 2, cols], start=False, stop=True)\
                  .then_inc(L3["v_ps"].sem, 1)

            def project(t, p, par):
                was = neighbours(t - 1, p + PAIRS - 2)
                pe.wait_ge(L3["turned"].sem, L3["turned"].nth(was[0], was[1] + 1))
                if p < 4:
                    pe.wait_ge(L3["rest"].sem, L3["rest"].nth(t, min(p + 2, 4)))
                else:
                    pe.wait_ge(L3["rest"].sem, L3["rest"].nth(t, 4))
                cols = slice(p * P, (p + 1) * P)
                for i in range(2):
                    ps = bank[p % 2][:, i * T:(i + 1) * T]
                    pe.matmul(ps, w_hi[:, i, cols], h_hi[:, par, :], start=True, stop=False)
                    pe.matmul(ps, w_hi[:, i, cols], h_lo[:, par, :], start=False, stop=False)
                    last = pe.matmul(ps, w_lo[:, i, cols], h_hi[:, par, :], start=False, stop=True)
                last.then_inc(L3["qk_ps"].sem, 1)

            def scores(t, h):
                p, side = h // 2, slice((h % 2) * DH, (h % 2 + 1) * DH)
                pe.wait_ge(L3["rope"].sem, L3["rope"].nth(t, p + 1))
                was = t - 1 + (h + H - 2) // H, (h + H - 2) % H
                pe.wait_ge(L3["exp"].sem, L3["exp"].nth(was[0], was[1] + 1))
                s = bank[2 + h % 2]
                q, k = qk[side, p % 4, 0, :], qk[side, p % 4, 1, :]
                pe.matmul(s[:, 0:P], q[:, 0:P], k[:, 0:P], start=True, stop=False)
                pe.matmul(s[:, 0:P], ident_bf[:, :], causal_bf[:, :], start=False, stop=True)
                pe.matmul(s[:, P:3 * P], q[:, P:T], k[:, :], start=True, stop=False)
                pe.matmul(s[:, 2 * P:3 * P], ident_bf[:, :], causal_bf[:, :], start=False, stop=True)\
                  .then_inc(L3["s"].sem, 1)

            def transpose_probs(t, h):
                pe.wait_ge(L3["exp"].sem, L3["exp"].nth(t, h + 1))
                was = t - 1 + (h + H - 2) // H, (h + H - 2) % H
                pe.wait_ge(L3["pT_lo"].sem, L3["pT_lo"].nth(was[0], was[1] + 1))
                for blk in range(3):
                    cols = slice(blk * P, (blk + 1) * P)
                    last = pe.transpose(bank[4 + h % 2][:, cols], probs[:, h % 4, cols], ident[:, :])
                last.then_inc(L3["pT"].sem, 1)

            def transpose_tiles(t):
                pe.wait_ge(L3["xn"].sem, L3["xn"].nth(t, 1))
                for j in range(NT):
                    last = pe.transpose(bank[4 + j][:, 3 * P:4 * P], xn[:, 0, j, :], ident[:, :])
                last.then_inc(L3["xT"].sem, 1)

            def weigh(t, h, par):
                pe.wait_ge(L3["pT_lo"].sem, L3["pT_lo"].nth(t, h + 1))
                if h == 0:
                    pe.wait_ge(L3["v3"].sem, L3["v3"].nth(t, 4))
                if h % 2 == 0:
                    was = neighbours(t - 1, h // 2 + PAIRS - 1)
                    pe.wait_ge(L3["oT"].sem, L3["oT"].nth(was[0], was[1] + 1))
                for j in range(NT):
                    at = (2 * j + h % 2) * (DH + 1)
                    wide = bank[6][:, at:at + DH + 1]
                    thin = bank[6][:, at:at + DH]
                    for kt in range(j + 1):
                        blk = slice((j + kt) * P, (j + kt + 1) * P)
                        hi, lo = probsT_hi[:, h % 4, blk], probsT_lo[:, h % 4, blk]
                        pe.matmul(wide, hi, val1[:, par, kt, h, :], start=(kt == 0), stop=False)
                        pe.matmul(thin, hi, val2[:, par, kt, h, :], start=False, stop=False)
                        pe.matmul(thin, hi, val3[:, par, kt, h, :], start=False, stop=False)
                        pe.matmul(wide, lo, val1[:, par, kt, h, :], start=False, stop=False)
                        last = pe.matmul(thin, lo, val2[:, par, kt, h, :], start=False, stop=(kt == j))
                if h % 2 == 1:
                    last.then_inc(L3["pv"].sem, 1)

            def heads_to_rows(t, p):
                pe.wait_ge(L3["o"].sem, L3["o"].nth(t, p + 1))
                for j in range(NT):
                    last = pe.transpose(bank[6][:, j * P:(j + 1) * P],
                                        o[:, p % 2, j, :, :].rearrange("p h d -> p (h d)"), ident[:, :])
                last.then_inc(L3["oT_ps"].sem, 1)

            def project_out(t, p):
                pe.wait_ge(L3["oT"].sem, L3["oT"].nth(t, p + 1))
                if p == 0:
                    pe.wait_ge(L3["gated"].sem, L3["gated"].before(t, 1))
                for j in range(NT):
                    last = pe.matmul(bank[7][:, j * P:(j + 1) * P], oT[:, p % 2, j * P:(j + 1) * P], woT[:, p, :],
                                     start=(p == 0 and j == 0), stop=(p == PAIRS - 1), skip_group_check=True)
                last.then_inc(L3["y_add"].sem, 1)

            def attend_row(t, par, more, start=False):
                for p in range(PAIRS):
                    if more and p == 1:
                        transpose_tiles(t + 1)
                    if not start:
                        if more and p == 2:
                            pe.wait_ge(L3["h"].sem, L3["h"].nth(t + 1, 1))
                        transpose_probs(t, 2 * p)
                        transpose_probs(t, 2 * p + 1)
                    if not start and p + 1 < PAIRS:
                        scores(t, 2 * p + 2)
                        scores(t, 2 * p + 3)
                    if more and p == PAIRS - 1:
                        scores(t + 1, 0)
                        scores(t + 1, 1)
                    if not start and p >= 1:
                        heads_to_rows(t, p - 1)
                    if not start and p + 3 < PAIRS:
                        project(t, p + 3, par)
                    if more and p + 3 >= PAIRS:
                        project(t + 1, p + 3 - PAIRS, 1 - par)
                    if more and 3 <= p < 7:
                        project_v(t + 1, p - 3, 1 - par)
                    if not start:
                        weigh(t, 2 * p, par)
                        weigh(t, 2 * p + 1, par)
                    if not start and p >= 1:
                        project_out(t, p - 1)
                if start:
                    return
                heads_to_rows(t, PAIRS - 1)
                project_out(t, PAIRS - 1)

            pe.wait_ge(w_split, 6)
            attend_row(-1, 1, True, start=True)
            with pe.Fori(0, B // 2 - 1) as i:
                attend_row(2 * i, 0, True)
                attend_row(2 * i + 1, 1, True)
            attend_row(B - 2, 0, True)
            attend_row(B - 1, 1, False)

            def gelu_ahead(t):
                for w in range(WIDE):
                    pe.wait_ge(L4["gated"].sem, L4["gated"].before(t, w + 1))
                    to_d_major(L4, t, w, w + 1, bank[4 + w])

            def up(t, w):
                pe.wait_ge(L4["h"].sem, L4["h"].nth(t, w + 1))
                if w >= 2:
                    pe.wait_ge(L4["act"].sem, L4["act"].nth(t, FC * (w - 1)))
                else:
                    pe.wait_ge(L4["act"].sem, L4["act"].before(t, FC * (w + 3)))
                for c in range(FC):
                    last = pe.matmul(bank[2 * (w % 2) + c // 2][:, (c % 2) * T:(c % 2 + 1) * T],
                                     uv1[:, c * P:(c + 1) * P], hT[:, w, :], start=True, stop=True)
                last.then_inc(L4["up"].sem, 1)

            def down(t, w):
                pe.wait_ge(L4["act"].sem, L4["act"].nth(t, FC * (w + 1)))
                for j in range(NT):
                    ps = bank[4 + w][:, j * P:(j + 1) * P]
                    for c in range(FC):
                        pe.matmul(ps, hid[:, w, c, j * P:(j + 1) * P], uv2[:, c, :], start=(c == 0), stop=False)
                    last = bias(ps, 2)
                last.then_inc(L4["y"].sem, 1)

            pe.wait_ge(L3["gated"].sem, L3["gated"].nth(B - 1, 1))
            with pe.Fori(0, B // WIDE) as t:
                gelu_ahead(t)
                up(t, 0)
                for w in range(1, WIDE):
                    up(t, w)
                    down(t, w - 1)
                down(t, WIDE - 1)


def constants():
    inv_freq = (1.0 / np.float32(10000.0) ** (np.arange(0, DH, 2, dtype=np.float32) / np.float32(DH))).astype(np.float32)
    angle = np.outer(np.arange(T, dtype=np.float32), inv_freq).astype(np.float32)
    cos, sin = np.cos(angle).T, np.sin(angle).T
    lo, hi = slice(0, HALF // 2), slice(HALF // 2, HALF)
    cos4 = np.concatenate([cos[lo], cos[lo], cos[hi], cos[hi]] * 2)
    sin4 = np.concatenate([-sin[lo], sin[lo], -sin[hi], sin[hi]] * 2)
    scale = np.float32(DH ** -0.5)
    rope = np.stack([cos4 * scale, cos4, sin4 * scale, sin4], axis=1).astype(np.float32)
    i = np.arange(P)
    causal = np.where(i[None, :] > i[:, None], np.float32(-1e30), np.float32(0))
    same = (i[:, None] // PICK == i[None, :] // PICK) & (i[:, None] < i[None, :])
    first = np.eye(P, dtype=np.float32) - 2 * same.astype(np.float32)
    return {"ident": np.eye(P, dtype=np.float32), "causal": causal.astype(np.float32), "first": first, "rope": rope}


def kernel(**inputs):
    import numpy as _np
    import concourse.bacc as _bacc
    from concourse import mybir as _mybir
    from concourse.bass_utils import run_bass_kernel_spmd as _run

    i = {k: _np.asarray(v) for k, v in inputs.items()}

    def paired(w):
        return w.reshape(H, 2, 2, HALF // 2, D).transpose(0, 2, 1, 3, 4).reshape(H * DH, D)

    wq, wk, wv = i["L1_attn_wq"], i["L1_attn_wk"], i["L1_attn_wv"]
    arrays = {
        "x": i["L0_attn_x"].reshape(TILES, P, D).transpose(1, 0, 2),
        "cT": _np.stack([i["L0_c"].T, i["L1_c"].T], axis=1),
        "wmod": _np.stack([i["L0_wmod"], i["L1_wmod"]], axis=1),
        "wg": i["L0_attn_Wg"].reshape(D, 1),
        "bg": i["L0_attn_bg"].reshape(1, 1),
        "woutT": i["L0_attn_Wout"].T,
        "rows": _np.concatenate([i["L0_ffn_mb"].reshape(F), i["L0_attn_bout"], i["L0_ffn_b2"], i["L1_ffn_b2"]])[None],
        "m1T": i["L0_ffn_m1"].T,
        "m2": i["L0_ffn_m2"].reshape(DH, F),
        "w1": i["L0_ffn_w1"].reshape(D, F),
        "w2": i["L0_ffn_w2"].transpose(1, 0, 2).reshape(FC, P, D).transpose(1, 0, 2),
        "w_attn": _np.stack([paired(wq).T, paired(wk).T, wv.T]),
        "woT": i["L1_attn_wo"].T.reshape(PAIRS, P, D).transpose(1, 0, 2),
        "u1T": i["L1_ffn_U1"].T,
        "v1": i["L1_ffn_V1"],
        "u2T": i["L1_ffn_U2"].T,
        "v2": i["L1_ffn_V2"],
        "b1": i["L1_ffn_b1"].reshape(FC, P).T,
        **constants(),
    }
    arrays = {f"in_{k}_dram": _np.ascontiguousarray(v) for k, v in arrays.items()}
    nc = _bacc.Bacc("TRN2", target_bir_lowering=False, num_devices=1)
    args = {k[3:-5]: nc.dram_tensor(k, v.shape, _mybir.dt.from_np(v.dtype), kind="ExternalInput").ap()
            for k, v in arrays.items()}
    out = nc.dram_tensor("out_0_dram", (P, TILES, D), F32, kind="ExternalOutput").ap()
    program(nc, args, out)
    r = _run(nc, [arrays], core_ids=[0])
    got = r.results[0]["out_0_dram"]
    return _np.ascontiguousarray(_np.asarray(got).transpose(1, 0, 2).reshape(B, T, D))
```

```python
from contextlib import ExitStack

import numpy as np
import concourse.bass as bass
from concourse import mybir

ALU = mybir.AluOpType
ACT = mybir.ActivationFunctionType
AX_X = mybir.AxisListType.X
F32 = mybir.dt.float32
F32R = mybir.dt.float32r
BF16 = mybir.dt.bfloat16

P = 128
B, T, D = 16, 256, 128
NT = T // P
TILES = B * NT
F = 512
FC = F // P
GROUPS, PICK = 8, 64
H, DH = 16, 64
HALF = DH // 2
PAIRS = H // 2
EPS = 1e-5
WIDE = 4
VAR_STEPS = 7
ROOT_STEPS = 12
LATE_ROWS = WIDE
EARLY, LATE_TILES = slice(0, (B - LATE_ROWS) * NT), slice((B - LATE_ROWS) * NT, TILES)
ROOT_BATCHES = [slice(0, TILES // 2), slice(TILES // 2, TILES)] + [EARLY, LATE_TILES] * 3
ROWS = F + 3 * D
GATE_STEPS = 7
SWAP = [(i + 16) % 32 for i in range(32)]
TURN_AT = 2
V_AT = PAIRS - 4


class Signal:

    def __init__(self, ctx, nc, name, per_batch):
        self.sem = ctx.enter_context(nc.semaphore(name))
        self.per = per_batch

    def nth(self, t, n):
        return t * self.per + (self.per + n)

    def before(self, t, n):
        return t * self.per + n


def program(nc, a, gates_dram, out):
    ctx = ExitStack()
    with ctx:
        def sb(name, shape, dt=F32):
            return ctx.enter_context(nc.sbuf_tensor(name, shape, dt))

        def sem(name):
            return ctx.enter_context(nc.semaphore(name))

        signals = []

        def sig(name, per):
            signals.append(Signal(ctx, nc, name, per))
            return signals[-1]

        bank = [ctx.enter_context(nc.psum_tensor(f"bank{i}", [P, 512], F32)) for i in range(8)]

        x = sb("x", [P, TILES, D])
        ident = sb("ident", [P, P])
        ident_bf = sb("ident_bf", [P, P], BF16)
        causal = sb("causal", [P, P])
        causal_bf = sb("causal_bf", [P, P], BF16)
        first = sb("first", [P, P])
        first_bf = sb("first_bf", [P, P], BF16)
        rope_tab = sb("rope_tab", [P, 4, T])
        ones3 = sb("ones3", [3, P], BF16)
        cT = sb("cT", [P, 2, B])
        silu = sb("silu", [P, 2, B])
        silu_e = sb("silu_e", [P, 2, B])
        wmod = sb("wmod", [P, 2, 6 * D])
        modT = sb("modT", [P, 2, 4, B])
        gate_row = sb("gate_row", [B, 2, 2, D])
        gate = sb("gate", [P, 2, 2, B, D])
        gates0 = gate[:, 0, :, :, :].rearrange("p k r d -> p (k r d)")
        wg = sb("wg", [P, 1])
        bg = sb("bg", [P, 1])
        minus_bg = sb("minus_bg", [P, 1])
        woutT = sb("woutT", [P, D])
        rows = sb("rows", [ROWS // P, P])
        rows_part = sb("rows_part", [ROWS // P, 3, P], BF16)
        rows3 = sb("rows3", [3, ROWS], BF16)
        m1T = sb("m1T", [DH, D])
        m2 = sb("m2", [DH, F])
        w_in = sb("w_in", [P, 2 * F])
        w_in_hi = sb("w_in_hi", [P, 2 * F], F32R)
        w_in_lo = sb("w_in_lo", [P, 2 * F], F32R)
        w2 = sb("w2", [P, FC, D])
        stage = sb("stage", [P, 3, H * DH])
        w_hi = sb("w_hi", [P, 3, H * DH], F32R)
        w_lo = sb("w_lo", [P, 3, H * DH], F32R)
        woT = sb("woT", [P, PAIRS, D])
        u1T = sb("u1T", [32, D])
        v1 = sb("v1", [32, F])
        u2T = sb("u2T", [32, F])
        v2 = sb("v2", [32, D])
        b1 = sb("b1", [P, FC])
        uv1 = sb("uv1", [P, F])
        uv2 = sb("uv2", [P, FC, D])

        stats = sb("stats", [P, TILES, 6])
        mean = sb("mean", [P, TILES])
        apart = sb("apart", [P, TILES])
        var = sb("var", [P, TILES])
        root = sb("root", [P, TILES])
        rstd = sb("rstd", [P, TILES])
        newton = sb("newton", [P, TILES])

        xn = sb("xn", [P, WIDE, NT, D])
        hT = sb("hT", [P, WIDE, T])
        hid = sb("hid", [P, WIDE, FC, T])
        hid_flat = hid[:, :, :, :].rearrange("p w c t -> p (w c t)")
        g, keep, gh, scanned = (hid[:, :, i, :] for i in range(4))
        step = sb("step", [P, WIDE, NT, D])

        h_hi = sb("h_hi", [P, 2, T], F32R)
        h_lo = sb("h_lo", [P, 2, T], F32R)
        top = sb("top", [P, NT, GROUPS])
        hits = sb("hits", [P, NT, F], BF16)
        hitsT = sb("hitsT", [P, FC, T], BF16)
        picked = sb("picked", [P, FC, T], BF16)

        val = sb("val", [P, 2, NT, H * DH])
        rope_a = sb("rope_a", [P, 2, 2 * T])
        rope_b = sb("rope_b", [P, 2, 2 * T])
        rope_s = stage[:, 1, :].rearrange("p (b n) -> p b n", b=2)
        gate_hi, gate_lo, gate_a, gate_b = (
            r[0:B, i, :].rearrange("b (l k d) -> b l k d", l=2, k=2) for r in (rope_a, rope_b) for i in range(2))
        up_hi, up_lo = (w_hi[:, i, :].rearrange("p (w t) -> p w t", w=WIDE) for i in range(2))
        uv1_hi, uv1_lo = w_in_hi[:, 0:F], w_in_hi[:, F:2 * F]
        nmax = sb("nmax", [P, 4, NT])
        rsum = sb("rsum", [P, 4, NT])
        inv = sb("inv", [P, 4, NT])
        qk = gates0[:, 0:2048].rearrange("p (b a t) -> p b a t", b=4, a=2)
        oT = gates0[:, 2048:2560].rearrange("p (b t) -> p b t", b=2)
        probs = hid_flat[:, 0:1536].rearrange("p (b k) -> p b k", b=4)
        probsT = hid_flat[:, 1536:3072].rearrange("p (b k) -> p b k", b=4)

        s_x = [sem(f"x_loaded_{i}") for i in range(2)]
        s_c = sem("conditions_loaded")
        s_mod = [sem(f"modulation_weights_loaded_{i}") for i in range(2)]
        s_const = sem("constants_loaded")
        s_late = sem("later_constants_loaded")
        s_rows = sem("bias_rows_spread")
        s_gate_out = sem("gates_stored")
        s_gate = [sem(f"gates_spread_{i}") for i in range(4)]
        s_out = sem("output_stored")
        pre_v = sem("prologue_vector")
        pre_s = sem("prologue_scalar")
        pre_t = sem("prologue_tensor")
        rows_step = sem("bias_rows_step")
        bg_turned = sem("minus_bg")
        gate_step = sem("gates_step")
        x_stats = sem("input_statistics")
        w_round = sem("attention_weight_rounded")
        w_split = sem("attention_weight_split")
        w_in_split = sem("feed_forward_weight_split")
        uv1_split = sem("fused_weight_split")
        st_v = sem("rstd_vector_step")
        st_s = sem("rstd_root")

        def phase(tag, **counts):
            return {k: sig(f"{tag}_{k}", v) for k, v in counts.items()}

        L1 = phase("scan", xn=WIDE, xT=WIDE, h=WIDE, z=WIDE, g=WIDE, keep=WIDE, gh=WIDE, scanned=WIDE,
                   y=WIDE, gated=WIDE, x=WIDE, stats=WIDE)
        L2 = phase("pick", xn=1, xT=1, h=1, hi=1, lo=1, logits=2, top=2, hits=2, hitsT_ps=1, hitsT=1,
                   first=1, picked=2, hidden=1, hid=2, y=1, gated=1, x=1, stats=1)
        L3 = phase("attn", xn=1, xT=1, h=1, hi=1, lo=1, v_ps=4, v=4, qk_ps=PAIRS, swapped=PAIRS, mul=PAIRS,
                   mul2=PAIRS, rope=PAIRS, s=H, nmax=H, exp=H, inv=H, scaled=H, pT_ps=H, pT=H,
                   oT_ps=PAIRS, oT=PAIRS, y_add=PAIRS, gated=1, x=1, stats=1)
        L3["y"] = L3["y_add"]
        L4 = phase("gelu", xn=WIDE, xT=WIDE, h=WIDE, hi=WIDE, lo=WIDE, up=WIDE, act=WIDE * FC, y=WIDE, gated=WIDE, x=WIDE)

        def full(tensor):
            return tensor[tuple(slice(None) for _ in tensor.shape)]

        CONSTS = [(full(dst), a[name]) for dst, name in (
            (ident, "ident"), (rows, "rows"), (wg, "wg"), (woutT, "woutT"), (m1T, "m1T"), (m2, "m2"),
            (u1T, "u1T"), (v1, "v1"), (u2T, "u2T"), (v2, "v2"), (first, "first"))]
        CONSTS += [(w_in[:, F:2 * F], a["w1"]), (bg[:, :], a["bg"].to_broadcast([P, 1]))]
        EARLY_CONSTS = 3
        LATE = [(full(dst), a[name]) for dst, name in (
            (causal, "causal"), (w2, "w2"), (b1, "b1"), (rope_tab, "rope"), (woT, "woT"))]
        LATE += [(full(stage), a["w_attn"].rearrange("a p n -> p a n"))]
        N_CONST, N_LATE = 16 * len(CONSTS), 16 * len(LATE)

        block = ctx.enter_context(nc.Block())

        @block.sync
        def _(sp):
            sp.dma_start(cT[:, :, :], a["cT"]).then_inc(s_c, 16)
            for i in range(2):
                sp.dma_start(wmod[:, i, :], a["wmod"][:, i, :]).then_inc(s_mod[i], 16)
                n = TILES // 2
                sp.dma_start(x[:, i * n:(i + 1) * n, :], a["x"][:, i * n:(i + 1) * n, :]).then_inc(s_x[i], 16)
            for s in signals:
                sp.sem_inc(s.sem, s.per)
            sp.wait_ge(rows_step, 5)
            for i in range(3):
                sp.dma_start(rows3[i:i + 1, :].rearrange("o (c n) -> o c n", n=P), rows_part[:, i, :])\
                  .then_inc(s_rows, 16)
            sp.wait_ge(gate_step, GATE_STEPS)
            sp.dma_start(gates_dram.rearrange("l k b d -> b l k d"), gate_row[:, :, :, :]).then_inc(s_gate_out, 16)
            sp.wait_ge(s_gate_out, 16)
            for n in range(4):
                l, k = n // 2, n % 2
                sp.dma_start(gate[:, l, k, :, :].rearrange("p b d -> p (b d)"),
                             gates_dram[l, k, :, :].rearrange("b d -> (b d)").unsqueeze(0).to_broadcast([P, B * D]))\
                  .then_inc(s_gate[n], 16)
            for dst, src in LATE:
                sp.dma_start(dst, src).then_inc(s_late, 16)
            with sp.Fori(0, B // WIDE) as t:
                sp.wait_ge(L4["x"].sem, L4["x"].nth(t, WIDE))
                sp.dma_start(out[:, bass.ds(t * (WIDE * NT), WIDE * NT), :],
                             x[:, bass.ds(t * (WIDE * NT), WIDE * NT), :]).then_inc(s_out, 16)
            sp.wait_ge(s_out, 16 * (B // WIDE))

        def row_tiles(t):
            return x[:, bass.ds(t * NT, NT), :]

        def ahead(t, n):
            return not isinstance(t, int) or t + n < B

        def started(t, n):
            return not isinstance(t, int) or t >= n

        def neighbours(t, p):
            return t + p // PAIRS, p % PAIRS

        @block.vector
        def _(dve):
            dve.memset(ones3[:, :], 1.0).then_inc(pre_v, 1)
            dve.wait_ge(pre_s, 1)
            dve.tensor_tensor(silu[:, :, :], cT[:, :, :], silu_e[:, :, :], ALU.mult).then_inc(pre_v, 1)
            def input_stats(half):
                dve.wait_ge(s_x[half], 16)
                for i in range(half * (TILES // 2), (half + 1) * (TILES // 2)):
                    dve.bn_stats(stats[:, i, :], x[:, i, :]).then_inc(x_stats, 1)
                dve.wait_ge(x_stats, (half + 1) * (TILES // 2))

            def root_step(ins, n, done, wait=True):
                ins.then_inc(st_v, 1)
                if wait:
                    dve.wait_ge(st_v, ROOT_STEPS * n + done)

            def find_variances(n):
                b = ROOT_BATCHES[n]
                m0, m1, v0, v1 = (stats[:, b, k] for k in (1, 4, 2, 5))
                root_step(dve.tensor_tensor(apart[:, b], m0, m1, ALU.subtract), n, 1, False)
                root_step(dve.tensor_tensor(mean[:, b], m0, m1, ALU.add), n, 2, False)
                root_step(dve.tensor_tensor(var[:, b], v0, v1, ALU.add), n, 3)
                root_step(dve.scalar_tensor_tensor(out=apart[:, b], in0=apart[:, b], scalar=0.25, in1=apart[:, b],
                                                   op0=ALU.mult, op1=ALU.mult), n, 4, False)
                root_step(dve.tensor_scalar(var[:, b], var[:, b], 1.0 / D, EPS, ALU.mult, ALU.add), n, 5)
                root_step(dve.tensor_scalar(mean[:, b], mean[:, b], 0.5, None, ALU.mult), n, 6, False)
                root_step(dve.tensor_tensor(var[:, b], var[:, b], apart[:, b], ALU.add), n, VAR_STEPS)

            def invert_roots(n):
                b = ROOT_BATCHES[n]
                dve.wait_ge(st_s, n + 1)
                root_step(dve.reciprocal(rstd[:, b], root[:, b]), n, 8)
                root_step(dve.tensor_tensor(newton[:, b], var[:, b], rstd[:, b], ALU.mult), n, 9)
                root_step(dve.tensor_tensor(newton[:, b], newton[:, b], rstd[:, b], ALU.mult), n, 10)
                root_step(dve.tensor_scalar(newton[:, b], newton[:, b], -0.5, 1.5, ALU.mult, ALU.add), n, 11)
                root_step(dve.tensor_tensor(rstd[:, b], rstd[:, b], newton[:, b], ALU.mult), n, ROOT_STEPS)

            def normalise(S, t, w, row, nth):
                dve.wait_ge(S["xT"].sem, S["xT"].before(t, nth))
                normalise_row(S, w, row)

            def normalise_picking(row, w):
                if started(row, 2):
                    dve.wait_ge(L2["xT"].sem, L2["xT"].before(row - 1, 1))
                normalise_row(L2, w, row)

            def normalise_row(S, w, row):
                for j in range(NT):
                    i = row * NT + j
                    last = dve.tensor_scalar(
                        xn[:, w, j, :], x[:, bass.ds(i, 1), :].rearrange("p o d -> p (o d)"),
                        mean[:, bass.ds(i, 1)], rstd[:, bass.ds(i, 1)], ALU.subtract, ALU.mult)
                last.then_inc(S["xn"].sem, 1)

            def modulate(S, t, w, row, nth, psum, l, k):
                dve.wait_ge(S["xT"].sem, S["xT"].nth(t, nth))
                dve.tensor_scalar(hT[:, w, :], psum[:, 0:T], modT[:, l, 2 * k + 1, bass.ds(row, 1)],
                                  modT[:, l, 2 * k, bass.ds(row, 1)], ALU.mult, ALU.add).then_inc(S["h"].sem, 1)

            def apply_gate(S, t, w, row, nth, psum, l, k, y=None):
                dve.wait_ge(S["y"].sem, S["y"].nth(t, y or nth))
                gate_bc = gate[:, l, k, bass.ds(row, 1), :].to_broadcast([P, NT, D])
                dve.tensor_tensor(step[:, w, :, :], psum.rearrange("p (j d) -> p j d", j=NT), gate_bc, ALU.mult)\
                   .then_inc(S["gated"].sem, 1)

            def add_step(S, t, w, row, nth):
                dve.wait_ge(S["gated"].sem, S["gated"].nth(t, nth))
                dve.tensor_tensor(row_tiles(row), row_tiles(row), step[:, w, :, :], ALU.add).then_inc(S["x"].sem, 1)

            def new_stats(S, t, row, nth):
                dve.wait_ge(S["x"].sem, S["x"].nth(t, nth))
                for j in range(NT):
                    i = row * NT + j
                    last = dve.bn_stats(stats[:, bass.ds(i, 1), :].rearrange("p o s -> p (o s)"),
                                        x[:, bass.ds(i, 1), :].rearrange("p o d -> p (o d)"))
                last.then_inc(S["stats"].sem, 1)

            def turn_tiles(t, behind):
                dve.wait_ge(L3["lo"].sem, L3["lo"].before(t, 1))
                dve.wait_ge(L3["xT"].sem, L3["xT"].nth(t, 1))
                if behind:
                    dve.wait_ge(L3["pT"].sem, L3["pT"].nth(t - 1, 2 * TURN_AT + 2))
                for j in range(NT):
                    last = dve.tensor_scalar(hT[:, 0, j * P:(j + 1) * P], bank[4 + j][:, 3 * P:4 * P],
                                             modT[:, 1, 1, bass.ds(t, 1)], modT[:, 1, 0, bass.ds(t, 1)],
                                             ALU.mult, ALU.add)
                last.then_inc(L3["h"].sem, 1)

            def scan_normalise(t):
                for w in range(WIDE):
                    normalise(L1, t, w, t * WIDE + w, w + 1)

            def scan_modulate(t):
                for w in range(WIDE):
                    dve.wait_ge(L1["z"].sem, L1["z"].before(t, w + 1))
                    dve.wait_ge(L1["gh"].sem, L1["gh"].before(t, w + 1))
                    modulate(L1, t, w, t * WIDE + w, w + 1, bank[2 * w + 1], 0, 0)

            def scan_stats(t):
                for w in range(WIDE):
                    new_stats(L1, t, t * WIDE + w, w + 1)

            def scan_group(t, more):
                if more:
                    scan_normalise(t + 1)
                else:
                    scan_stats(t - 1)
                    dve.wait_ge(L1["stats"].sem, L1["stats"].before(t, WIDE))
                    find_variances(2)
                for w in range(WIDE):
                    dve.wait_ge(L1["keep"].sem, L1["keep"].nth(t, w + 1))
                    dve.wait_ge(L1["gh"].sem, L1["gh"].nth(t, w + 1))
                    dve.wait_ge(L1["y"].sem, L1["y"].before(t, w + 1))
                    dve.tensor_tensor_scan(scanned[:, w, :], keep[:, w, :], gh[:, w, :], 0.0,
                                           ALU.mult, ALU.add).then_inc(L1["scanned"].sem, 1)
                if more:
                    scan_modulate(t + 1)
                else:
                    invert_roots(2)
                    for row in range(2):
                        normalise_picking(row, row)
                dve.wait_ge(s_gate[0], 16)
                for w in range(WIDE):
                    dve.wait_ge(L1["x"].sem, L1["x"].before(t, w + 1))
                    apply_gate(L1, t, w, t * WIDE + w, w + 1, bank[2 * w][:, 0:T], 0, 0)
                    if w == 1 and more and started(t, 1):
                        scan_stats(t - 1)

            input_stats(0)
            find_variances(0)
            invert_roots(0)
            scan_normalise(0)

            def layer_modulations(l):
                dve.wait_ge(pre_t, l + 1)
                for k in range(4):
                    dve.tensor_scalar(modT[:, l, k, :], bank[0][:, (l * 4 + k) * B:(l * 4 + k + 1) * B],
                                      float(k % 2), None, ALU.add).then_inc(pre_v, 1)
                dve.wait_ge(pre_v, 2 + 4 * (l + 1))

            layer_modulations(0)
            dve.wait_ge(s_const, N_CONST)
            dve.tensor_scalar(minus_bg[:, :], bg[:, :], -1.0, None, ALU.mult).then_inc(bg_turned, 1)
            for i in range(3):
                dve.tensor_copy(rows_part[:, i, :], rows[:, :]).then_inc(rows_step, 1)
                if i < 2:
                    dve.wait_ge(rows_step, 2 * i + 1)
                    dve.tensor_tensor(rows[:, :], rows[:, :], rows_part[:, i, :], ALU.subtract)\
                       .then_inc(rows_step, 1)
                    dve.wait_ge(rows_step, 2 * i + 2)
            scan_modulate(0)
            layer_modulations(1)
            input_stats(1)
            find_variances(1)
            scan_group(0, True)
            invert_roots(1)
            with dve.Fori(1, B // WIDE - 1) as t:
                scan_group(t, True)
            scan_group(B // WIDE - 1, False)
            scan_stats(B // WIDE - 1)
            dve.wait_ge(L1["stats"].sem, L1["stats"].nth(B // WIDE - 1, WIDE))

            def find_hits(t, j):
                groups = bank[1 + j][:, :].rearrange("p (g k) -> p g k", g=GROUPS)
                dve.wait_ge(L2["logits"].sem, L2["logits"].nth(t, j + 1))
                dve.tensor_reduce(top[:, j, :], groups, AX_X, ALU.max).then_inc(L2["top"].sem, 1)
                dve.wait_ge(L2["hitsT_ps"].sem, L2["hitsT_ps"].before(t, 1))
                dve.wait_ge(L2["top"].sem, L2["top"].nth(t, j + 1))
                dve.tensor_tensor(hits[:, j, :].rearrange("p (g k) -> p g k", g=GROUPS), groups,
                                  top[:, j, :].unsqueeze(2).to_broadcast([P, GROUPS, PICK]),
                                  ALU.is_ge).then_inc(L2["hits"].sem, 1)

            def pick_row(t, par):
                if ahead(t, 1):
                    for j in range(NT):
                        find_hits(t + 1, j)
                for c2 in range(2):
                    dve.wait_ge(L2["hidden"].sem, L2["hidden"].nth(t, 1))
                    dve.wait_ge(L2["picked"].sem, L2["picked"].nth(t, c2 + 1))
                    if started(t, 2):
                        dve.wait_ge(L2["y"].sem, L2["y"].before(t - 1, 1))
                    dve.scalar_tensor_tensor(
                        out=hid[:, par, 2 * c2:2 * c2 + 2, :].rearrange("p c t -> p (c t)"),
                        in0=bank[6 + c2][:, :], scalar=0.0,
                        in1=picked[:, 2 * c2:2 * c2 + 2, :].rearrange("p c t -> p (c t)"),
                        op0=ALU.max, op1=ALU.mult).then_inc(L2["hid"].sem, 1)
                if started(t, 1):
                    apply_gate(L2, t - 1, 1 - par, t - 1, 1, bank[3][:, 0:T], 0, 1)
                if ahead(t, 3):
                    normalise_picking(t + 3, 1 - par)
                if started(t, 2):
                    new_stats(L2, t - 2, t - 2, 1)

            normalise_picking(2, 0)
            for j in range(NT):
                find_hits(0, j)
            find_variances(3)
            pick_row(0, 0)
            invert_roots(3)
            dve.wait_ge(s_gate[1], 16)
            pick_row(1, 1)
            with dve.Fori(1, B // 2 - 2) as i:
                pick_row(2 * i, 0)
                pick_row(2 * i + 1, 1)
            for t in range(B - 4, B):
                pick_row(t, t % 2)
                if t == B - 3:
                    dve.wait_ge(L2["stats"].sem, L2["stats"].nth(B - 1 - LATE_ROWS, 1))
                    find_variances(4)
                if t == B - 2:
                    invert_roots(4)
                    normalise(L3, 0, 0, 0, 1)
            turn_tiles(0, False)
            apply_gate(L2, B - 1, 1, B - 1, 1, bank[3][:, 0:T], 0, 1)
            for t in (B - 2, B - 1):
                new_stats(L2, t, t, 1)
            dve.wait_ge(L2["stats"].sem, L2["stats"].nth(B - 1, 1))

            def rotate_ready(t, p):
                dve.wait_ge(L3["qk_ps"].sem, L3["qk_ps"].nth(t, p + 1))
                was = neighbours(t - 1, p + PAIRS - 2)
                dve.wait_ge(L3["rope"].sem, L3["rope"].nth(was[0], was[1] + 1))

            def rotate_swap(t, p):
                dve.stream_shuffle(rope_s[:, p % 2, :], bank[p % 2][:, :], SWAP).then_inc(L3["swapped"].sem, 1)

            def rotate_cos(t, p):
                dve.tensor_tensor(rope_a[:, p % 2, :], bank[p % 2][:, :],
                                  rope_tab[:, 0:2, :].rearrange("p a t -> p (a t)"), ALU.mult)\
                   .then_inc(L3["mul"].sem, 1)

            def row_max(t, h):
                s = bank[2 + h % 2]
                dve.wait_ge(L3["s"].sem, L3["s"].nth(t, h + 1))
                was = t - 1 + (h + H - 4) // H, (h + H - 4) % H
                dve.wait_ge(L3["exp"].sem, L3["exp"].nth(was[0], was[1] + 1))
                dve.tensor_reduce(nmax[:, h % 4, 0:1], s[:, 0:P], AX_X, ALU.max, negate=True)
                dve.tensor_reduce(nmax[:, h % 4, 1:2], s[:, P:3 * P], AX_X, ALU.max, negate=True)\
                   .then_inc(L3["nmax"].sem, 1)

            def divide(t, h, swap=()):
                b = h % 4
                for row, pair in swap:
                    rotate_ready(row, pair)
                dve.wait_ge(L3["exp"].sem, L3["exp"].nth(t, h + 1))
                dve.reciprocal(inv[:, b, :], rsum[:, b, :]).then_inc(L3["inv"].sem, 1)
                for row, pair in swap:
                    rotate_swap(row, pair)
                dve.wait_ge(L3["inv"].sem, L3["inv"].nth(t, h + 1))
                dve.tensor_scalar(probs[:, b, 0:P], probs[:, b, 0:P], inv[:, b, 0:1], None, ALU.mult)
                dve.tensor_scalar(probs[:, b, P:3 * P], probs[:, b, P:3 * P], inv[:, b, 1:2], None, ALU.mult)\
                   .then_inc(L3["scaled"].sem, 1)

            def attend_first():
                for p in range(2):
                    rotate_ready(0, p)
                    rotate_swap(0, p)
                    rotate_cos(0, p)
                find_variances(5)
                for h in range(2):
                    row_max(0, h)
                for h in range(2):
                    divide(0, h, [(0, 2)] if h == 0 else [])

            def attend_row(t, par, more):
                def later(n):
                    row, pair = neighbours(t, p + n)
                    return [(row, pair)] if more or p + n < PAIRS else []

                for p in range(PAIRS):
                    for row, pair in later(1):
                        row_max(row, 2 * pair)
                    for row, pair in later(2):
                        rotate_cos(row, pair)
                    if more and p == TURN_AT - 1:
                        normalise(L3, t + 1, 0, t + 1, 1)
                    for row, pair in later(1):
                        row_max(row, 2 * pair + 1)
                    for row, pair in later(1):
                        divide(row, 2 * pair, later(3))
                        divide(row, 2 * pair + 1)
                    if started(t, 1):
                        if p == 0:
                            apply_gate(L3, t - 1, 0, t - 1, 1, bank[7][:, 0:T], 1, 0, y=PAIRS)
                        if p == 1:
                            add_step(L3, t - 1, 0, t - 1, 1)
                        if p == 3:
                            new_stats(L3, t - 1, t - 1, 1)
                    if more and p == TURN_AT:
                        turn_tiles(t + 1, True)

            dve.wait_ge(s_late, N_LATE)
            attend_first()
            invert_roots(5)
            dve.wait_ge(s_gate[2], 16)
            attend_row(0, 0, True)
            attend_row(1, 1, True)
            with dve.Fori(1, B // 2 - 1) as i:
                attend_row(2 * i, 0, True)
                attend_row(2 * i + 1, 1, True)
            attend_row(B - 2, 0, True)
            dve.wait_ge(L3["stats"].sem, L3["stats"].nth(B - 1 - LATE_ROWS, 1))
            find_variances(6)
            attend_row(B - 1, 1, False)

            def gelu_normalise(t, rows=range(WIDE)):
                for w in rows:
                    normalise(L4, t, w, t * WIDE + w, w + 1)

            def gelu_modulate(t, w):
                dve.wait_ge(L4["up"].sem, L4["up"].before(t, w + 1))
                dve.wait_ge(L4["lo"].sem, L4["lo"].before(t, w + 1))
                dve.wait_ge(L4["xT"].sem, L4["xT"].nth(t, w + 1))
                row = t * WIDE + w
                shift, scale = modT[:, 1, 2, bass.ds(row, 1)], modT[:, 1, 3, bass.ds(row, 1)]
                for part, name in ((up_hi, "hi"), (hT, "h")):
                    dve.tensor_scalar(part[:, w, :], bank[4 + w][:, 0:T], scale, shift, ALU.mult, ALU.add)\
                       .then_inc(L4[name].sem, 1)

            def gelu_group(t, more):
                for w in (2, 3):
                    gelu_modulate(t, w)
                if more:
                    gelu_normalise(t + 1)
                for w in range(3):
                    apply_gate(L4, t, w, t * WIDE + w, w + 1, bank[4 + w][:, 0:T], 1, 1)
                if more:
                    for w in (0, 1):
                        gelu_modulate(t + 1, w)
                for w in range(3):
                    add_step(L4, t, w, t * WIDE + w, w + 1)
                apply_gate(L4, t, 3, t * WIDE + 3, 4, bank[7][:, 0:T], 1, 1)
                add_step(L4, t, 3, t * WIDE + 3, 4)

            invert_roots(6)
            gelu_normalise(0, range(2))
            gelu_modulate(0, 0)
            apply_gate(L3, B - 1, 0, B - 1, 1, bank[7][:, 0:T], 1, 0, y=PAIRS)
            add_step(L3, B - 1, 0, B - 1, 1)
            gelu_modulate(0, 1)
            new_stats(L3, B - 1, B - 1, 1)
            gelu_normalise(0, range(2, WIDE))
            dve.wait_ge(L3["stats"].sem, L3["stats"].nth(B - 1, 1))
            find_variances(7)
            invert_roots(7)
            dve.wait_ge(s_gate[3], 16)
            with dve.Fori(0, B // WIDE - 1) as t:
                gelu_group(t, True)
            gelu_group(B // WIDE - 1, False)

        @block.scalar
        def _(act):
            for dst, src in CONSTS[:EARLY_CONSTS]:
                act.dma_start(dst, src).then_inc(s_const, 16)
            act.wait_ge(s_c, 16)
            act.activation(silu_e[:, :, :], cT[:, :, :], ACT.Sigmoid).then_inc(pre_s, 1)
            for dst, src in CONSTS[EARLY_CONSTS:]:
                act.dma_start(dst, src).then_inc(s_const, 16)

            def roots(n):
                act.wait_ge(st_v, ROOT_STEPS * n + VAR_STEPS)
                act.activation(root[:, ROOT_BATCHES[n]], var[:, ROOT_BATCHES[n]], ACT.Sqrt).then_inc(st_s, 1)

            act.wait_ge(pre_t, 2)
            act.activation(gate_row[:, :, :, :], bank[1][0:B, :].rearrange("b (l k d) -> b l k d", l=2, k=2), ACT.Copy)\
               .then_inc(pre_s, 1)
            roots(0)
            act.wait_ge(pre_t, 3)
            act.activation(w_in[:, 0:F], bank[2][:, :], ACT.Copy).then_inc(pre_s, 1)
            act.wait_ge(pre_s, 3)
            act.activation(w_in_hi[:, :], w_in[:, :], ACT.Copy).then_inc(w_in_split, 1)
            act.wait_ge(bg_turned, 1)
            def scan_gates(t):
                for w in range(WIDE):
                    act.wait_ge(L1["z"].sem, L1["z"].nth(t, w + 1))
                    act.wait_ge(L1["gh"].sem, L1["gh"].before(t, w + 1))
                    act.wait_ge(L1["scanned"].sem, L1["scanned"].before(t, w + 1))
                    act.activation(g[:, w, :], bank[2 * w + 1][:, 0:T], ACT.Sigmoid, bias=bg[:, 0:1])\
                       .then_inc(L1["g"].sem, 1)
                    act.activation(keep[:, w, :], bank[2 * w + 1][:, 0:T], ACT.Sigmoid, bias=minus_bg[:, 0:1],
                                   scale=-1.0).then_inc(L1["keep"].sem, 1)

            scan_gates(0)
            act.wait_ge(pre_t, 4)
            act.activation(uv1[:, :], bank[4][:, :], ACT.Copy).then_inc(pre_s, 1)
            act.activation(uv2[:, :, :], bank[6][:, :].rearrange("p (c d) -> p c d", c=FC), ACT.Copy)\
               .then_inc(pre_s, 1)
            roots(1)
            with act.Fori(1, B // WIDE) as t:
                scan_gates(t)

            def modulate_split(t, par):
                act.wait_ge(L2["xT"].sem, L2["xT"].nth(t, 1))
                act.wait_ge(L2["lo"].sem, L2["lo"].before(t, 1))
                if started(t, 1):
                    act.wait_ge(L2["hidden"].sem, L2["hidden"].before(t - 1, 1))
                shift, scale = modT[:, 0, 2, bass.ds(t, 1)], modT[:, 0, 3, bass.ds(t, 1)]
                act.activation(hT[:, 0, :], bank[0][:, 0:T], ACT.Identity, bias=shift, scale=scale)\
                   .then_inc(L2["h"].sem, 1)
                act.activation(h_hi[:, par, :], bank[0][:, 0:T], ACT.Identity, bias=shift, scale=scale)\
                   .then_inc(L2["hi"].sem, 1)

            def pick_row(t, par):
                act.wait_ge(L2["hitsT_ps"].sem, L2["hitsT_ps"].nth(t, 1))
                act.wait_ge(L2["first"].sem, L2["first"].before(t, 1))
                act.activation(hitsT[:, :, :].rearrange("p c t -> p (c t)"), bank[3][:, :].bitcast(BF16), ACT.Copy)\
                   .then_inc(L2["hitsT"].sem, 1)
                if ahead(t, 2):
                    modulate_split(t + 2, par)
                act.wait_ge(L2["first"].sem, L2["first"].nth(t, 1))
                for c2 in range(2):
                    act.wait_ge(L2["hid"].sem, L2["hid"].before(t, c2 + 1))
                    act.activation(picked[:, 2 * c2:2 * c2 + 2, :].rearrange("p c t -> p (c t)"),
                                   bank[4 + c2][:, :], ACT.Relu).then_inc(L2["picked"].sem, 1)

            def round_weights(i):
                act.activation(w_hi[:, i, :], stage[:, i, :], ACT.Copy).then_inc(w_round, 1)

            roots(2)
            modulate_split(0, 0)
            act.wait_ge(s_late, N_LATE)
            round_weights(0)
            modulate_split(1, 1)
            pick_row(0, 0)
            roots(3)
            round_weights(1)
            pick_row(1, 1)
            round_weights(2)
            with act.Fori(1, B // 2 - 2) as i:
                pick_row(2 * i, 0)
                pick_row(2 * i + 1, 1)
            for t in range(B - 4, B):
                pick_row(t, t % 2)
                if t == B - 3:
                    roots(4)

            def v_out(t, u, par, b):
                act.wait_ge(L3["v_ps"].sem, L3["v_ps"].nth(t, u + 1))
                act.activation(val[:, par, u // 2, (u % 2) * 512:(u % 2 + 1) * 512], bank[b][:, :], ACT.Copy)\
                   .then_inc(L3["v"].sem, 1)

            def probs_out(t, h):
                act.wait_ge(L3["pT_ps"].sem, L3["pT_ps"].nth(t, h + 1))
                was = neighbours(t - 1, h // 2 + PAIRS - 2)
                act.wait_ge(L3["oT_ps"].sem, L3["oT_ps"].nth(was[0], was[1] + 1))
                act.activation(probsT[:, h % 4, :], bank[4 + h % 2][:, 0:3 * P], ACT.Copy)\
                   .then_inc(L3["pT"].sem, 1)

            def exps(t, h):
                s = bank[2 + h % 2]
                act.wait_ge(L3["nmax"].sem, L3["nmax"].nth(t, h + 1))
                was = t - 1 + (h + H - 4) // H, (h + H - 4) % H
                act.wait_ge(L3["pT_ps"].sem, L3["pT_ps"].nth(was[0], was[1] + 1))
                act.activation(probs[:, h % 4, 0:P], s[:, 0:P], ACT.Exp, bias=nmax[:, h % 4, 0:1],
                               accum_out=rsum[:, h % 4, 0:1])
                act.activation(probs[:, h % 4, P:3 * P], s[:, P:3 * P], ACT.Exp, bias=nmax[:, h % 4, 1:2],
                               accum_out=rsum[:, h % 4, 1:2]).then_inc(L3["exp"].sem, 1)

            def heads_out(t, p):
                act.wait_ge(L3["oT_ps"].sem, L3["oT_ps"].nth(t, p + 1))
                was = neighbours(t - 1, p + PAIRS - 2)
                act.wait_ge(L3["y_add"].sem, L3["y_add"].nth(was[0], was[1] + 1))
                act.activation(oT[:, p % 2, :], bank[6][:, 0:T], ACT.Copy).then_inc(L3["oT"].sem, 1)

            def round_h(t, par):
                act.wait_ge(L3["h"].sem, L3["h"].nth(t, 1))
                act.wait_ge(L3["qk_ps"].sem, L3["qk_ps"].before(t, 1))
                act.activation(h_hi[:, par, :], hT[:, 0, :], ACT.Copy).then_inc(L3["hi"].sem, 1)

            def attend_row(t, par, more):
                for p in range(PAIRS):
                    if p >= 1:
                        heads_out(t, p - 1)
                    elif started(t, 1):
                        heads_out(t - 1, PAIRS - 1)
                    for side in range(2):
                        probs_out(t, 2 * p + side)
                        if p + 1 < PAIRS:
                            exps(t, 2 * p + 2 + side)
                        elif more:
                            exps(t + 1, side)
                        if more and p == TURN_AT + 1 and side == 0:
                            round_h(t + 1, 1 - par)
                    if more and p >= V_AT:
                        v_out(t + 1, p - V_AT, 1 - par, (p - V_AT) % 2)

            round_h(0, 0)
            for u in range(4):
                v_out(0, u, 0, 4 + u)
            roots(5)
            for h in range(2):
                exps(0, h)
            attend_row(0, 0, True)
            attend_row(1, 1, True)
            with act.Fori(1, B // 2 - 1) as i:
                attend_row(2 * i, 0, True)
                attend_row(2 * i + 1, 1, True)
            attend_row(B - 2, 0, True)
            attend_row(B - 1, 1, False)
            roots(6)
            heads_out(B - 1, PAIRS - 1)
            act.activation(uv1_hi, uv1[:, :], ACT.Copy).then_inc(uv1_split, 1)
            roots(7)
            with act.Fori(0, B // WIDE) as t:
                for w in range(WIDE):
                    act.wait_ge(L4["y"].sem, L4["y"].before(t, w + 1))
                    act.wait_ge(L4["up"].sem, L4["up"].nth(t, w + 1))
                    for c in range(FC):
                        act.activation(hid[:, w, c, :], bank[2 * (w % 2) + c // 2][:, (c % 2) * T:(c % 2 + 1) * T],
                                       ACT.Gelu_apprx_tanh, bias=b1[:, c:c + 1]).then_inc(L4["act"].sem, 1)

        @block.gpsimd
        def _(pool):
            pool.wait_ge(pre_s, 2)
            g_row = gate_row[:, :, :, :]
            pool.tensor_scalar(gate_hi, g_row, 0.25, None, ALU.max).then_inc(gate_step, 1)
            pool.tensor_scalar(gate_lo, g_row, -0.25, None, ALU.min).then_inc(gate_step, 1)
            pool.tensor_scalar(gate_a, g_row, 0.0, None, ALU.is_ge).then_inc(gate_step, 1)
            pool.tensor_scalar(gate_b, g_row, 0.0, None, ALU.is_lt).then_inc(gate_step, 1)
            pool.wait_ge(gate_step, 4)
            pool.tensor_tensor(gate_a, gate_a, gate_hi, ALU.mult).then_inc(gate_step, 1)
            pool.tensor_tensor(gate_b, gate_b, gate_lo, ALU.mult).then_inc(gate_step, 1)
            pool.wait_ge(gate_step, 6)
            pool.tensor_tensor(g_row, gate_a, gate_b, ALU.add).then_inc(gate_step, 1)
            pool.wait_ge(s_const, N_CONST)
            pool.tensor_copy(ident_bf[:, :], ident[:, :]).then_inc(w_in_split, 1)
            pool.tensor_copy(first_bf[:, :], first[:, :]).then_inc(w_in_split, 1)

            def scan_products(t):
                for w in range(WIDE):
                    pool.wait_ge(L1["g"].sem, L1["g"].nth(t, w + 1))
                    pool.wait_ge(L1["scanned"].sem, L1["scanned"].before(t, w + 1))
                    pool.tensor_tensor(gh[:, w, :], g[:, w, :], hT[:, w, :], ALU.mult).then_inc(L1["gh"].sem, 1)

            def scan_adds(t, rows):
                for w in rows:
                    pool.wait_ge(L1["gated"].sem, L1["gated"].nth(t, w + 1))
                    row = row_tiles(t * WIDE + w)
                    pool.tensor_tensor(row, row, step[:, w, :, :], ALU.add).then_inc(L1["x"].sem, 1)

            scan_products(0)
            scan_adds(0, range(WIDE))
            pool.wait_ge(w_in_split, 3)
            pool.tensor_tensor(w_in_lo[:, :], w_in[:, :], w_in_hi[:, :].bitcast(F32), ALU.subtract)\
                .then_inc(w_in_split, 1)
            with pool.Fori(1, B // WIDE - 1) as t:
                scan_products(t)
                scan_adds(t, range(WIDE))
            scan_products(B // WIDE - 1)
            scan_adds(B // WIDE - 1, range(2))

            def split_picking(t, par):
                pool.wait_ge(L2["hi"].sem, L2["hi"].nth(t, 1))
                if started(t, 1):
                    pool.wait_ge(L2["hidden"].sem, L2["hidden"].before(t - 1, 1))
                pool.tensor_tensor(h_lo[:, par, :], hT[:, 0, :], h_hi[:, par, :].bitcast(F32), ALU.subtract)\
                    .then_inc(L2["lo"].sem, 1)

            def add_picked(t, par):
                pool.wait_ge(L2["gated"].sem, L2["gated"].nth(t, 1))
                pool.tensor_tensor(row_tiles(t), row_tiles(t), step[:, par, :, :], ALU.add).then_inc(L2["x"].sem, 1)

            split_picking(0, 0)
            scan_adds(B // WIDE - 1, range(2, WIDE))
            split_picking(1, 1)
            for t in range(4):
                split_picking(t + 2, t % 2)
                if t >= 1:
                    add_picked(t - 1, 1 - t % 2)
                    pool.wait_ge(w_round, t)
                    pool.tensor_tensor(w_lo[:, t - 1, :], stage[:, t - 1, :], w_hi[:, t - 1, :].bitcast(F32),
                                       ALU.subtract).then_inc(w_split, 1)
            pool.tensor_copy(causal_bf[:, :], causal[:, :]).then_inc(w_split, 1)
            with pool.Fori(2, B // 2 - 1) as i:
                for par in range(2):
                    split_picking(2 * i + par + 2, par)
                    add_picked(2 * i + par - 1, 1 - par)
            for t in range(B - 3, B - 1):
                add_picked(t, t % 2)

            def rope(t, p):
                pool.wait_ge(L3["swapped"].sem, L3["swapped"].nth(t, p + 1))
                pool.tensor_tensor(rope_b[:, p % 2, :], rope_s[:, p % 2, :],
                                   rope_tab[:, 2:4, :].rearrange("p a t -> p (a t)"), ALU.mult)\
                    .then_inc(L3["mul2"].sem, 1)
                pool.wait_ge(L3["mul2"].sem, L3["mul2"].nth(t, p + 1))
                pool.wait_ge(L3["mul"].sem, L3["mul"].nth(t, p + 1))
                was = neighbours(t - 1, p + PAIRS - 4)
                pool.wait_ge(L3["s"].sem, L3["s"].nth(was[0], 2 * was[1] + 2))
                pool.tensor_tensor(qk[:, p % 4, :, :].rearrange("p a t -> p (a t)"), rope_a[:, p % 2, :],
                                   rope_b[:, p % 2, :], ALU.add).then_inc(L3["rope"].sem, 1)

            def split_h(t, par):
                pool.wait_ge(L3["h"].sem, L3["h"].nth(t, 1))
                pool.wait_ge(L3["hi"].sem, L3["hi"].nth(t, 1))
                pool.tensor_tensor(h_lo[:, par, :], hT[:, 0, :], h_hi[:, par, :].bitcast(F32), ALU.subtract)\
                    .then_inc(L3["lo"].sem, 1)

            def attend_row(t, par, more):
                for p in range(PAIRS):
                    if more and p == TURN_AT + 1:
                        split_h(t + 1, 1 - par)
                    if p + 3 < PAIRS:
                        rope(t, p + 3)
                    elif more:
                        rope(t + 1, p + 3 - PAIRS)

            split_h(0, 0)
            add_picked(B - 1, 1)
            for p in range(3):
                rope(0, p)
            attend_row(0, 0, True)
            attend_row(1, 1, True)
            with pool.Fori(1, B // 2 - 1) as i:
                attend_row(2 * i, 0, True)
                attend_row(2 * i + 1, 1, True)
            attend_row(B - 2, 0, True)
            attend_row(B - 1, 1, False)

            pool.wait_ge(uv1_split, 1)
            pool.tensor_tensor(uv1_lo, uv1[:, :], uv1_hi.bitcast(F32), ALU.subtract).then_inc(uv1_split, 1)
            with pool.Fori(0, B // WIDE) as t:
                for w in range(WIDE):
                    pool.wait_ge(L4["hi"].sem, L4["hi"].nth(t, w + 1))
                    pool.wait_ge(L4["h"].sem, L4["h"].nth(t, w + 1))
                    pool.wait_ge(L4["up"].sem, L4["up"].before(t, w + 1))
                    pool.tensor_tensor(up_lo[:, w, :], hT[:, w, :], up_hi[:, w, :].bitcast(F32), ALU.subtract)\
                        .then_inc(L4["lo"].sem, 1)

        @block.tensor
        def _(pe):
            pe.wait_ge(pre_v, 2)
            for l in range(2):
                pe.wait_ge(s_mod[l], 16)
                for k, part in enumerate((0, 1, 3, 4)):
                    pe.matmul(bank[0][:, (l * 4 + k) * B:(l * 4 + k + 1) * B],
                              wmod[:, l, part * D:(part + 1) * D], silu[:, l, :], start=True, stop=True)
                for k, part in enumerate((2, 5)):
                    last = pe.matmul(bank[1][0:B, (l * 2 + k) * D:(l * 2 + k + 1) * D], silu[:, l, :],
                                     wmod[:, l, part * D:(part + 1) * D], start=True, stop=True)
                last.then_inc(pre_t, 1)
            pe.wait_ge(s_const, N_CONST)
            pe.matmul(bank[2][:, :], m1T[:, :], m2[:, :], start=True, stop=True).then_inc(pre_t, 1)

            def to_d_major(S, t, w, nth, psum):
                pe.wait_ge(S["xn"].sem, S["xn"].nth(t, nth))
                for j in range(NT):
                    last = pe.transpose(psum[:, j * P:(j + 1) * P], xn[:, w, j, :], ident[:, :])
                last.then_inc(S["xT"].sem, 1)

            def transpose_tiles(t):
                pe.wait_ge(L3["xn"].sem, L3["xn"].nth(t, 1))
                for j in range(NT):
                    last = pe.transpose(bank[4 + j][:, 3 * P:4 * P], xn[:, 0, j, :], ident[:, :])
                last.then_inc(L3["xT"].sem, 1)

            def bias(psum, k):
                return pe.matmul(psum, ones3[:, :], rows3[:, F + k * D:F + (k + 1) * D], start=False, stop=True)

            def scan_ahead(t):
                for w in range(WIDE):
                    pe.wait_ge(L1["keep"].sem, L1["keep"].before(t, w + 1))
                    to_d_major(L1, t, w, w + 1, bank[2 * w + 1])

            def scan_sums(t):
                for w in range(WIDE):
                    pe.wait_ge(L1["h"].sem, L1["h"].nth(t, w + 1))
                    pe.matmul(bank[2 * w + 1][:, 0:T], wg[:, 0:1].to_broadcast([P, P]), hT[:, w, :],
                              start=True, stop=True).then_inc(L1["z"].sem, 1)

            def scan_out(t):
                for w in range(WIDE):
                    pe.wait_ge(L1["gated"].sem, L1["gated"].before(t, w + 1))
                    pe.wait_ge(L1["scanned"].sem, L1["scanned"].nth(t, w + 1))
                    for j in range(NT):
                        ps = bank[2 * w][:, j * P:(j + 1) * P]
                        pe.matmul(ps, scanned[:, w, j * P:(j + 1) * P], woutT[:, :], start=True, stop=False)
                        last = bias(ps, 0)
                    last.then_inc(L1["y"].sem, 1)

            pe.wait_ge(pre_s, 2)
            scan_ahead(0)
            scan_sums(0)
            pe.matmul(bank[4][:, :], u1T[:, :], v1[:, :], start=True, stop=True)
            for c in range(FC):
                last = pe.matmul(bank[6][:, c * D:(c + 1) * D], u2T[:, c * P:(c + 1) * P], v2[:, :],
                                 start=True, stop=True)
            last.then_inc(pre_t, 1)
            scan_ahead(1)
            pe.wait_ge(pre_v, 10)
            pe.wait_ge(pre_s, 5)
            pe.wait_ge(s_rows, 48)
            scan_out(0)
            with pe.Fori(1, B // WIDE - 1) as t:
                scan_sums(t)
                scan_ahead(t + 1)
                scan_out(t)
            scan_sums(B // WIDE - 1)
            scan_out(B // WIDE - 1)

            def find_logits(t, par):
                pe.wait_ge(L2["hi"].sem, L2["hi"].nth(t, 1))
                pe.wait_ge(L2["lo"].sem, L2["lo"].nth(t, 1))
                for j in range(NT):
                    tok = slice(j * P, (j + 1) * P)
                    ps = bank[1 + j][:, :]
                    pe.wait_ge(L2["hits"].sem, L2["hits"].before(t, j + 1))
                    pe.matmul(ps, h_hi[:, par, tok], w_in_hi[:, 0:F], start=True, stop=False)
                    pe.matmul(ps, h_hi[:, par, tok], w_in_lo[:, 0:F], start=False, stop=False)
                    pe.matmul(ps, h_lo[:, par, tok], w_in_hi[:, 0:F], start=False, stop=False)
                    pe.matmul(ps, ones3[:, :], rows3[:, 0:F], start=False, stop=True)\
                      .then_inc(L2["logits"].sem, 1)

            def find_hidden(t, par):
                for c in range(FC):
                    if c % 2 == 0:
                        pe.wait_ge(L2["hid"].sem, L2["hid"].before(t, c // 2 + 1))
                    f = slice(F + c * P, F + (c + 1) * P)
                    ps = bank[6 + c // 2][:, (c % 2) * T:(c % 2 + 1) * T]
                    pe.matmul(ps, w_in_hi[:, f], h_hi[:, par, :], start=True, stop=False)
                    pe.matmul(ps, w_in_hi[:, f], h_lo[:, par, :], start=False, stop=False)
                    last = pe.matmul(ps, w_in_lo[:, f], h_hi[:, par, :], start=False, stop=True)
                last.then_inc(L2["hidden"].sem, 1)

            def pick_row(t, par):
                hits_ps = bank[3][:, :].bitcast(BF16)
                if ahead(t, 1):
                    find_logits(t + 1, 1 - par)
                if started(t, 2):
                    pe.wait_ge(L2["gated"].sem, L2["gated"].before(t - 1, 1))
                else:
                    pe.wait_ge(L2["hitsT"].sem, L2["hitsT"].before(t, 1))
                for j in range(NT):
                    pe.wait_ge(L2["hits"].sem, L2["hits"].nth(t, j + 1))
                    for c in range(FC):
                        last = pe.transpose(hits_ps[:, c * T + j * P:c * T + (j + 1) * P],
                                            hits[:, j, c * P:(c + 1) * P], ident_bf[:, :])
                last.then_inc(L2["hitsT_ps"].sem, 1)
                find_hidden(t, par)
                if ahead(t, 2):
                    pe.wait_ge(L2["hi"].sem, L2["hi"].nth(t + 1, 1))
                    to_d_major(L2, t + 2, par, 1, bank[0])
                pe.wait_ge(L2["hitsT"].sem, L2["hitsT"].nth(t, 1))
                pe.wait_ge(L2["picked"].sem, L2["picked"].before(t, 2))
                for c in range(FC):
                    last = pe.matmul(bank[4 + c // 2][:, (c % 2) * T:(c % 2 + 1) * T], first_bf[:, :],
                                     hitsT[:, c, :], start=True, stop=True)
                last.then_inc(L2["first"].sem, 1)
                if started(t, 1):
                    feed_out(t - 1, 1 - par)

            def feed_out(t, par):
                pe.wait_ge(L2["hitsT"].sem, L2["hitsT"].nth(t + 1 if ahead(t, 1) else t, 1))
                pe.wait_ge(L2["hid"].sem, L2["hid"].nth(t, 2))
                for j in range(NT):
                    ps = bank[3][:, j * P:(j + 1) * P]
                    for c in range(FC):
                        pe.matmul(ps, hid[:, par, c, j * P:(j + 1) * P], w2[:, c, :], start=(c == 0), stop=False)
                    last = bias(ps, 1)
                last.then_inc(L2["y"].sem, 1)

            pe.wait_ge(L1["gated"].sem, L1["gated"].nth(B // WIDE - 1, 1))
            to_d_major(L2, 0, 0, 1, bank[0])
            pe.wait_ge(L2["hi"].sem, L2["hi"].nth(0, 1))
            to_d_major(L2, 1, 1, 1, bank[0])
            pe.wait_ge(w_in_split, 4)
            pe.wait_ge(s_late, N_LATE)
            pe.wait_ge(L1["gated"].sem, L1["gated"].nth(B // WIDE - 1, 2))
            find_logits(0, 0)
            pe.wait_ge(L1["gated"].sem, L1["gated"].nth(B // WIDE - 1, WIDE))
            pick_row(0, 0)
            pick_row(1, 1)
            with pe.Fori(1, B // 2 - 2) as i:
                pick_row(2 * i, 0)
                pick_row(2 * i + 1, 1)
            for t in range(B - 4, B):
                pick_row(t, t % 2)
            pe.wait_ge(L2["picked"].sem, L2["picked"].nth(B - 1, 2))
            transpose_tiles(0)
            pe.wait_ge(L2["gated"].sem, L2["gated"].nth(B - 2, 1))
            feed_out(B - 1, 1)

            def project_v(t, u, par, b):
                tok = slice(u // 2 * P, (u // 2 + 1) * P)
                cols = slice((u % 2) * 512, (u % 2 + 1) * 512)
                if u == 0:
                    pe.wait_ge(L3["lo"].sem, L3["lo"].nth(t, 1))
                if b < 2:
                    was = neighbours(t - 1, u + V_AT + 2)
                    pe.wait_ge(L3["swapped"].sem, L3["swapped"].nth(was[0], was[1] + 1))
                    pe.wait_ge(L3["mul"].sem, L3["mul"].nth(was[0], was[1] + 1))
                ps = bank[b][:, :]
                pe.matmul(ps, h_hi[:, par, tok], w_hi[:, 2, cols], start=True, stop=False)
                pe.matmul(ps, h_hi[:, par, tok], w_lo[:, 2, cols], start=False, stop=False)
                pe.matmul(ps, h_lo[:, par, tok], w_hi[:, 2, cols], start=False, stop=True)\
                  .then_inc(L3["v_ps"].sem, 1)

            def project(t, p, par):
                was = neighbours(t - 1, p + PAIRS - 2)
                pe.wait_ge(L3["swapped"].sem, L3["swapped"].nth(was[0], was[1] + 1))
                pe.wait_ge(L3["mul"].sem, L3["mul"].nth(was[0], was[1] + 1))
                if p < 4 and started(t, 1):
                    pe.wait_ge(L3["v"].sem, L3["v"].nth(t, p + 1))
                cols = slice(p * P, (p + 1) * P)
                for i in range(2):
                    ps = bank[p % 2][:, i * T:(i + 1) * T]
                    pe.matmul(ps, w_hi[:, i, cols], h_hi[:, par, :], start=True, stop=False)
                    pe.matmul(ps, w_hi[:, i, cols], h_lo[:, par, :], start=False, stop=False)
                    last = pe.matmul(ps, w_lo[:, i, cols], h_hi[:, par, :], start=False, stop=True)
                last.then_inc(L3["qk_ps"].sem, 1)

            def scores(t, h):
                p, side = h // 2, slice((h % 2) * DH, (h % 2 + 1) * DH)
                pe.wait_ge(L3["rope"].sem, L3["rope"].nth(t, p + 1))
                was = t - 1 + (h + H - 2) // H, (h + H - 2) % H
                pe.wait_ge(L3["exp"].sem, L3["exp"].nth(was[0], was[1] + 1))
                s = bank[2 + h % 2]
                q, k = qk[side, p % 4, 0, :], qk[side, p % 4, 1, :]
                pe.matmul(s[:, 0:P], q[:, 0:P], k[:, 0:P], start=True, stop=False, skip_group_check=True)
                pe.matmul(s[:, P:3 * P], q[:, P:T], k[:, :], start=False, stop=False, skip_group_check=True)
                pe.matmul(s[:, 0:4 * P].rearrange("p (b k) -> p b k", b=2)[:, :, 0:P], ident_bf[:, :],
                          causal_bf[:, :].unsqueeze(1).to_broadcast([P, 2, P]), start=False, stop=True,
                          skip_group_check=True).then_inc(L3["s"].sem, 1)

            def transpose_probs(t, h):
                pe.wait_ge(L3["scaled"].sem, L3["scaled"].nth(t, h + 1))
                was = t - 1 + (h + H - 2) // H, (h + H - 2) % H
                pe.wait_ge(L3["pT"].sem, L3["pT"].nth(was[0], was[1] + 1))
                for blk in range(3):
                    cols = slice(blk * P, (blk + 1) * P)
                    last = pe.transpose(bank[4 + h % 2][:, cols], probs[:, h % 4, cols], ident[:, :])
                last.then_inc(L3["pT_ps"].sem, 1)

            def weigh(t, p, par):
                if p == 0:
                    pe.wait_ge(L3["v"].sem, L3["v"].nth(t, 4))
                was = neighbours(t - 1, p + PAIRS - 1)
                pe.wait_ge(L3["oT"].sem, L3["oT"].nth(was[0], was[1] + 1))
                pe.wait_ge(L3["pT"].sem, L3["pT"].nth(t, 2 * p + 2))
                for kt in range(NT):
                    for h in (2 * p, 2 * p + 1):
                        side = slice((h % 2) * DH, (h % 2 + 1) * DH)
                        last = pe.matmul(bank[6][side, kt * P:T], val[:, par, kt, h * DH:(h + 1) * DH],
                                         probsT[:, h % 4, 2 * kt * P:(2 + kt) * P], start=(kt == 0), stop=(kt == 1),
                                         skip_group_check=True)
                last.then_inc(L3["oT_ps"].sem, 1)

            def project_out(t, p):
                pe.wait_ge(L3["oT"].sem, L3["oT"].nth(t, p + 1))
                if p == 0:
                    pe.wait_ge(L3["gated"].sem, L3["gated"].before(t, 1))
                for j in range(NT):
                    last = pe.matmul(bank[7][:, j * P:(j + 1) * P], oT[:, p % 2, j * P:(j + 1) * P], woT[:, p, :],
                                     start=(p == 0 and j == 0), stop=(p == PAIRS - 1), skip_group_check=True)
                last.then_inc(L3["y_add"].sem, 1)

            def attend_row(t, par, more):
                for p in range(PAIRS):
                    for side in range(2):
                        if p + 1 < PAIRS:
                            scores(t, 2 * p + 2 + side)
                        elif more:
                            scores(t + 1, side)
                        if more and p == TURN_AT and side == 0:
                            transpose_tiles(t + 1)
                        if more and p == TURN_AT + 1 and side == 0:
                            pe.wait_ge(L3["h"].sem, L3["h"].nth(t + 1, 1))
                        transpose_probs(t, 2 * p + side)
                    if p + 3 < PAIRS:
                        project(t, p + 3, par)
                    elif more:
                        project(t + 1, p + 3 - PAIRS, 1 - par)
                    if more and p >= V_AT:
                        project_v(t + 1, p - V_AT, 1 - par, (p - V_AT) % 2)
                    if p >= 1:
                        project_out(t, p - 1)
                    elif started(t, 1):
                        project_out(t - 1, PAIRS - 1)
                    weigh(t, p, par)

            pe.wait_ge(w_split, 4)
            pe.wait_ge(L3["lo"].sem, L3["lo"].nth(0, 1))
            project(0, 0, 0)
            project(0, 1, 0)
            for u in range(4):
                project_v(0, u, 0, 4 + u)
            project(0, 2, 0)
            scores(0, 0)
            scores(0, 1)
            pe.wait_ge(L3["v"].sem, L3["v"].nth(0, 4))
            attend_row(0, 0, True)
            attend_row(1, 1, True)
            with pe.Fori(1, B // 2 - 1) as i:
                attend_row(2 * i, 0, True)
                attend_row(2 * i + 1, 1, True)
            attend_row(B - 2, 0, True)
            attend_row(B - 1, 1, False)
            project_out(B - 1, PAIRS - 1)

            def gelu_turn(t, w):
                pe.wait_ge(L4["gated"].sem, L4["gated"].before(t, w + 1))
                to_d_major(L4, t, w, w + 1, bank[4 + w])

            def up(t, w):
                pe.wait_ge(L4["hi"].sem, L4["hi"].nth(t, w + 1))
                pe.wait_ge(L4["lo"].sem, L4["lo"].nth(t, w + 1))
                pe.wait_ge(L4["h"].sem, L4["h"].nth(t, w + 1))
                if w >= 2:
                    pe.wait_ge(L4["act"].sem, L4["act"].nth(t, FC * (w - 1)))
                else:
                    pe.wait_ge(L4["act"].sem, L4["act"].before(t, FC * (w + 3)))
                for c in range(FC):
                    ps, f = bank[2 * (w % 2) + c // 2][:, (c % 2) * T:(c % 2 + 1) * T], slice(c * P, (c + 1) * P)
                    pe.matmul(ps, uv1_hi[:, f], up_hi[:, w, :], start=True, stop=False)
                    pe.matmul(ps, uv1_hi[:, f], up_lo[:, w, :], start=False, stop=False)
                    last = pe.matmul(ps, uv1_lo[:, f], up_hi[:, w, :], start=False, stop=True)
                last.then_inc(L4["up"].sem, 1)

            def down(t, w):
                pe.wait_ge(L4["act"].sem, L4["act"].nth(t, FC * (w + 1)))
                for j in range(NT):
                    ps = bank[4 + w][:, j * P:(j + 1) * P]
                    for c in range(FC):
                        pe.matmul(ps, hid[:, w, c, j * P:(j + 1) * P], uv2[:, c, :], start=(c == 0), stop=False)
                    last = bias(ps, 2)
                last.then_inc(L4["y"].sem, 1)

            def gelu_group(t, more):
                up(t, 0)
                for w in (2, 3):
                    gelu_turn(t, w)
                for w in range(1, WIDE):
                    up(t, w)
                    down(t, w - 1)
                if more:
                    for w in (0, 1):
                        gelu_turn(t + 1, w)
                down(t, WIDE - 1)

            for w in (0, 1):
                gelu_turn(0, w)
            pe.wait_ge(uv1_split, 2)
            pe.wait_ge(L3["gated"].sem, L3["gated"].nth(B - 1, 1))
            with pe.Fori(0, B // WIDE - 1) as t:
                gelu_group(t, True)
            gelu_group(B // WIDE - 1, False)


def constants():
    inv_freq = (1.0 / np.float32(10000.0) ** (np.arange(0, DH, 2, dtype=np.float32) / np.float32(DH))).astype(np.float32)
    angle = np.outer(np.arange(T, dtype=np.float32), inv_freq).astype(np.float32)
    cos, sin = np.cos(angle).T, np.sin(angle).T
    lo, hi = slice(0, HALF // 2), slice(HALF // 2, HALF)
    cos4 = np.concatenate([cos[lo], cos[lo], cos[hi], cos[hi]] * 2)
    sin4 = np.concatenate([-sin[lo], sin[lo], -sin[hi], sin[hi]] * 2)
    scale = np.float32(DH ** -0.5)
    rope = np.stack([cos4 * scale, cos4, sin4 * scale, sin4], axis=1).astype(np.float32)
    i = np.arange(P)
    causal = np.where(i[None, :] > i[:, None], np.float32(-1e30), np.float32(0))
    same = (i[:, None] // PICK == i[None, :] // PICK) & (i[:, None] < i[None, :])
    first = np.eye(P, dtype=np.float32) - 2 * same.astype(np.float32)
    return {"ident": np.eye(P, dtype=np.float32), "causal": causal.astype(np.float32), "first": first, "rope": rope}


def kernel(**inputs):
    import numpy as _np
    import concourse.bacc as _bacc
    from concourse import mybir as _mybir
    from concourse.bass_utils import run_bass_kernel_spmd as _run

    i = {k: _np.asarray(v) for k, v in inputs.items()}

    def paired(w):
        return w.reshape(H, 2, 2, HALF // 2, D).transpose(0, 2, 1, 3, 4).reshape(H * DH, D)

    wq, wk, wv = i["L1_attn_wq"], i["L1_attn_wk"], i["L1_attn_wv"]
    arrays = {
        "x": i["L0_attn_x"].reshape(TILES, P, D).transpose(1, 0, 2),
        "cT": _np.stack([i["L0_c"].T, i["L1_c"].T], axis=1),
        "wmod": _np.stack([i["L0_wmod"], i["L1_wmod"]], axis=1),
        "wg": i["L0_attn_Wg"].reshape(D, 1),
        "bg": i["L0_attn_bg"].reshape(1, 1),
        "woutT": i["L0_attn_Wout"].T,
        "rows": _np.concatenate([i["L0_ffn_mb"].reshape(F), i["L0_attn_bout"], i["L0_ffn_b2"], i["L1_ffn_b2"]]).reshape(-1, P),
        "m1T": i["L0_ffn_m1"].T,
        "m2": i["L0_ffn_m2"].reshape(DH, F),
        "w1": i["L0_ffn_w1"].reshape(D, F),
        "w2": i["L0_ffn_w2"].transpose(1, 0, 2).reshape(FC, P, D).transpose(1, 0, 2),
        "w_attn": _np.stack([paired(wq).T, paired(wk).T, wv.T]),
        "woT": i["L1_attn_wo"].T.reshape(PAIRS, P, D).transpose(1, 0, 2),
        "u1T": i["L1_ffn_U1"].T,
        "v1": i["L1_ffn_V1"],
        "u2T": i["L1_ffn_U2"].T,
        "v2": i["L1_ffn_V2"],
        "b1": i["L1_ffn_b1"].reshape(FC, P).T,
        **constants(),
    }
    arrays = {f"in_{k}_dram": _np.ascontiguousarray(v) for k, v in arrays.items()}
    nc = _bacc.Bacc("TRN2", target_bir_lowering=False, num_devices=1)
    args = {k[3:-5]: nc.dram_tensor(k, v.shape, _mybir.dt.from_np(v.dtype), kind="ExternalInput").ap()
            for k, v in arrays.items()}
    out = nc.dram_tensor("out_0_dram", (P, TILES, D), F32, kind="ExternalOutput").ap()
    gates = nc.dram_tensor("gates_scratch", (2, 2, B, D), F32, kind="Internal").ap()
    program(nc, args, gates, out)
    r = _run(nc, [arrays], core_ids=[0])
    got = r.results[0]["out_0_dram"]
    return _np.ascontiguousarray(_np.asarray(got).transpose(1, 0, 2).reshape(B, T, D))
```
